# Optimizing a Trainium2 kernel written in Bass

```python
import numpy as np
import jax
import jax.numpy as jnp

def _softmax(x, axis=-1):
    return jax.nn.softmax(x, axis=axis)

def _gelu(x):
    return jax.nn.gelu(x, approximate=True)

def _silu(x):
    return jax.nn.silu(x)

def _sigmoid(x):
    return jax.nn.sigmoid(x)

def _layernorm(x, axis=-1, eps=1e-05):
    m = jnp.mean(x, axis=axis, keepdims=True)
    v = jnp.var(x, axis=axis, keepdims=True)
    return (x - m) / jnp.sqrt(v + eps)

def _scatter_add(tgt, idx, src, axis=0):
    return tgt.at[idx].add(src)

def _segment_sum(src, seg, n):
    return jax.ops.segment_sum(src, seg, n)
kernel_name = 'mk_vit_tower_cls_d2_tok_img256_r4_4430fb'

def setup_inputs(seed: int=0):
    np.random.seed(seed)
    _w = jnp.asarray

    def _rec_inputs():
        import jax
        import jax.numpy as jnp
        _rk = jax.random.key(seed)
        x = -0.000395706 + 0.999959 * jax.random.normal(jax.random.fold_in(_rk, 1), (32, 1, 224, 224), jnp.float32)
        cls_tok = 0.02 * jax.random.normal(jax.random.fold_in(_rk, 5), (1, 1, 64), jnp.float32)
        return (x, cls_tok)
    x, cls_tok = _rec_inputs()

    def _L0_tok_setup():
        import jax, jax.numpy as jnp
        import numpy as np
        IMAGE_SIZE = 224
        PATCH_SIZE = 7
        EMBED_DIM = 64
        NUM_PATCHES = (IMAGE_SIZE // PATCH_SIZE) ** 2
        PATCH_DIM = PATCH_SIZE ** 2
        key = jax.random.key(seed)
        kx, kw, kb, kp = jax.random.split(key, 4)
        x = jax.random.normal(kx, (64, 1, IMAGE_SIZE, IMAGE_SIZE), dtype=jnp.float32)
        bound = 1.0 / np.sqrt(PATCH_DIM)
        W = jax.random.uniform(kw, (EMBED_DIM, PATCH_DIM), minval=-bound, maxval=bound, dtype=jnp.float32)
        b = jax.random.uniform(kb, (EMBED_DIM,), minval=-bound, maxval=bound, dtype=jnp.float32)
        pos = jax.random.uniform(kp, (1, NUM_PATCHES, EMBED_DIM), dtype=jnp.float32)
        return {'x': x, 'W': W, 'b': b, 'pos': pos}
    _L0_tok_all = _L0_tok_setup()
    _L0_tok_in = {k: v for k, v in _L0_tok_all.items() if k in ('W', 'b', 'pos')}
    del _L0_tok_all

    def _L0_attn_setup():
        import jax, jax.numpy as jnp
        import numpy as np
        GROUPS = 64
        EPS = 1e-05
        DIM = 64
        SEQ = 256
        BATCH = 1

        def _group_norm(y, weight, bias):
            g = y.reshape(y.shape[:-1] + (GROUPS, -1))
            mean = g.mean(axis=-1, keepdims=True)
            var = g.var(axis=-1, keepdims=True)
            g = (g - mean) * jax.lax.rsqrt(var + EPS)
            return g.reshape(y.shape) * weight + bias

        def gate_loop_operator(k, v, q, a):
            kv = (k[..., :, None] * v[..., None, :]).astype(a.dtype)
            aa = a[..., :, None]

            def binop(e_i, e_j):
                a_i, kv_i = e_i
                a_j, kv_j = e_j
                return (a_j * a_i, a_j * kv_i + kv_j)
            _, y = jax.lax.associative_scan(binop, (aa, kv), axis=1)
            y = jnp.real(y).astype(k.dtype)
            return jnp.einsum('bld,blde->ble', q, y)
        key = jax.random.key(seed)
        ks = jax.random.split(key, 7)
        ortho = jax.nn.initializers.orthogonal()
        return {'x': jax.random.normal(ks[0], (BATCH, SEQ, DIM), jnp.float32), 'wq': ortho(ks[1], (DIM, DIM), jnp.float32), 'wk': ortho(ks[2], (DIM, DIM), jnp.float32), 'wv': ortho(ks[3], (DIM, DIM), jnp.float32), 'wa': ortho(ks[4], (DIM, 2 * DIM), jnp.float32), 'wg': ortho(ks[5], (DIM, DIM), jnp.float32), 'wo': ortho(ks[6], (DIM, DIM), jnp.float32), 'gn_weight': jnp.ones((DIM,), jnp.float32), 'gn_bias': jnp.zeros((DIM,), jnp.float32), 'bias': jnp.zeros((DIM,), jnp.float32)}
    _L0_attn_all = _L0_attn_setup()
    _L0_attn_in = {k: v for k, v in _L0_attn_all.items() if k in ('wq', 'wk', 'wv', 'wa', 'wg', 'wo', 'gn_weight', 'gn_bias', 'bias')}
    del _L0_attn_all

    def _L0_ffn_setup():
        import jax, jax.numpy as jnp
        import numpy as np
        B, S, D = (8, 1024, 64)
        H = 4 * D
        CAPACITY = 0.5
        key = jax.random.key(seed)
        ks = jax.random.split(key, 6)
        x = jax.random.normal(ks[0], (B, S, D), dtype=jnp.float32)
        attention_mask = jnp.zeros((B, 1, 1, S), dtype=jnp.float32)
        wr = jax.random.normal(ks[1], (D, 1), dtype=jnp.float32) * 0.02
        br = jnp.zeros((1,), dtype=jnp.float32)
        w1 = jax.random.normal(ks[2], (D, H), dtype=jnp.float32) * 0.02
        b1 = jnp.zeros((H,), dtype=jnp.float32)
        w2 = jax.random.normal(ks[3], (H, D), dtype=jnp.float32) * 0.02
        b2 = jnp.zeros((D,), dtype=jnp.float32)
        return {'x': x, 'attention_mask': attention_mask, 'wr': wr, 'br': br, 'w1': w1, 'b1': b1, 'w2': w2, 'b2': b2}
    _L0_ffn_all = _L0_ffn_setup()
    _L0_ffn_in = {k: v for k, v in _L0_ffn_all.items() if k in ('attention_mask', 'wr', 'br', 'w1', 'b1', 'w2', 'b2')}
    del _L0_ffn_all

    def _L1_attn_setup():
        import jax, jax.numpy as jnp
        import numpy as np
        SEQ, BATCH, IN, HID = (512, 64, 64, 64)
        key = jax.random.key(seed)
        k1, k2, k3, k4, k5 = jax.random.split(key, 5)
        s = 1.0 / np.sqrt(HID)
        return {'x_in': jax.random.normal(k1, (SEQ, BATCH, IN), dtype=jnp.float32), 'W_ih': jax.random.uniform(k2, (HID, IN), jnp.float32, -s, s), 'W_hh': jax.random.uniform(k3, (HID, HID), jnp.float32, -s, s), 'b_ih': jax.random.uniform(k4, (HID,), jnp.float32, -s, s), 'b_hh': jax.random.uniform(k5, (HID,), jnp.float32, -s, s)}
    _L1_attn_all = _L1_attn_setup()
    _L1_attn_in = {k: v for k, v in _L1_attn_all.items() if k in ('W_ih', 'W_hh', 'b_ih', 'b_hh')}
    del _L1_attn_all

    def _L1_ffn_setup():
        import jax, jax.numpy as jnp
        import numpy as np
        B, T, C = (64, 96, 64)
        NH, NKV = (4, 2)
        HD = C // NH
        NREP = NH // NKV
        NE, TOPK = (8, 2)
        HID = int(8 / 3 * C)
        EPS_RMS = 1e-06

        def _rope_tables(t_len):
            inv_freq = 1.0 / 10000.0 ** (np.arange(0, HD, 2, dtype=np.float32) / HD)
            t = np.arange(t_len, dtype=np.float32)
            freqs = np.outer(t, inv_freq)
            emb = np.concatenate([freqs, freqs], axis=-1)
            return (jnp.asarray(np.cos(emb)), jnp.asarray(np.sin(emb)))

        def _rotate_half(x):
            h = x.shape[-1] // 2
            return jnp.concatenate([-x[..., h:], x[..., :h]], axis=-1)

        def _rmsnorm(v, w):
            return v * jax.lax.rsqrt(jnp.mean(v * v, axis=-1, keepdims=True) + EPS_RMS) * w
        key = jax.random.key(seed)
        ks = jax.random.split(key, 10)
        s = lambda k, shape: jax.random.normal(k, shape, jnp.float32) * 0.02
        return {'x': jax.random.normal(ks[0], (B, T, C), jnp.float32), 'ln1_w': jnp.ones((C,), jnp.float32), 'ln2_w': jnp.ones((C,), jnp.float32), 'wq': s(ks[1], (NH * HD, C)), 'wk': s(ks[2], (NKV * HD, C)), 'wv': s(ks[3], (NKV * HD, C)), 'wo': s(ks[4], (C, C)), 'router_w': s(ks[5], (NE, C)), 'w1': s(ks[6], (NE, HID, C)), 'w2': s(ks[7], (NE, C, HID)), 'w3': s(ks[8], (NE, HID, C))}
    _L1_ffn_all = _L1_ffn_setup()
    _L1_ffn_in = {k: v for k, v in _L1_ffn_all.items() if k in ('ln1_w', 'ln2_w', 'wq', 'wk', 'wv', 'wo', 'router_w', 'w1', 'w2', 'w3')}
    del _L1_ffn_all
    return {'x': x, 'cls_tok': cls_tok, 'L0_tok_W': _L0_tok_in['W'], 'L0_tok_b': _L0_tok_in['b'], 'L0_tok_pos': _L0_tok_in['pos'], 'L0_attn_wq': _L0_attn_in['wq'], 'L0_attn_wk': _L0_attn_in['wk'], 'L0_attn_wv': _L0_attn_in['wv'], 'L0_attn_wa': _L0_attn_in['wa'], 'L0_attn_wg': _L0_attn_in['wg'], 'L0_attn_wo': _L0_attn_in['wo'], 'L0_attn_gn_weight': _L0_attn_in['gn_weight'], 'L0_attn_gn_bias': _L0_attn_in['gn_bias'], 'L0_attn_bias': _L0_attn_in['bias'], 'L0_ffn_attention_mask': _L0_ffn_in['attention_mask'], 'L0_ffn_wr': _L0_ffn_in['wr'], 'L0_ffn_br': _L0_ffn_in['br'], 'L0_ffn_w1': _L0_ffn_in['w1'], 'L0_ffn_b1': _L0_ffn_in['b1'], 'L0_ffn_w2': _L0_ffn_in['w2'], 'L0_ffn_b2': _L0_ffn_in['b2'], 'L1_attn_W_ih': _L1_attn_in['W_ih'], 'L1_attn_W_hh': _L1_attn_in['W_hh'], 'L1_attn_b_ih': _L1_attn_in['b_ih'], 'L1_attn_b_hh': _L1_attn_in['b_hh'], 'L1_ffn_ln1_w': _L1_ffn_in['ln1_w'], 'L1_ffn_ln2_w': _L1_ffn_in['ln2_w'], 'L1_ffn_wq': _L1_ffn_in['wq'], 'L1_ffn_wk': _L1_ffn_in['wk'], 'L1_ffn_wv': _L1_ffn_in['wv'], 'L1_ffn_wo': _L1_ffn_in['wo'], 'L1_ffn_router_w': _L1_ffn_in['router_w'], 'L1_ffn_w1': _L1_ffn_in['w1'], 'L1_ffn_w2': _L1_ffn_in['w2'], 'L1_ffn_w3': _L1_ffn_in['w3']}

def reference(x, cls_tok, L0_tok_W, L0_tok_b, L0_tok_pos, L0_attn_wq, L0_attn_wk, L0_attn_wv, L0_attn_wa, L0_attn_wg, L0_attn_wo, L0_attn_gn_weight, L0_attn_gn_bias, L0_attn_bias, L0_ffn_attention_mask, L0_ffn_wr, L0_ffn_br, L0_ffn_w1, L0_ffn_b1, L0_ffn_w2, L0_ffn_b2, L1_attn_W_ih, L1_attn_W_hh, L1_attn_b_ih, L1_attn_b_hh, L1_ffn_ln1_w, L1_ffn_ln2_w, L1_ffn_wq, L1_ffn_wk, L1_ffn_wv, L1_ffn_wo, L1_ffn_router_w, L1_ffn_w1, L1_ffn_w2, L1_ffn_w3):
    import jax
    import jax.numpy as jnp

    def _L0_tok_ref(x, W, b, pos):
        import jax, jax.numpy as jnp
        import numpy as np
        IMAGE_SIZE = 224
        PATCH_SIZE = 7
        EMBED_DIM = 64
        NUM_PATCHES = (IMAGE_SIZE // PATCH_SIZE) ** 2
        PATCH_DIM = PATCH_SIZE ** 2
        B = x.shape[0]
        p = PATCH_SIZE
        n = IMAGE_SIZE // p
        patches = x.reshape(B, n, p, n, p).transpose(0, 1, 3, 2, 4).reshape(B, n * n, p * p)
        out = jnp.einsum('bnd,ed->bne', patches, W) + b + pos
        return out

    def _L0_attn_ref(x, wq, wk, wv, wa, wg, wo, gn_weight, gn_bias, bias):
        import jax, jax.numpy as jnp
        import numpy as np
        GROUPS = 64
        EPS = 1e-05
        DIM = 64
        SEQ = 256
        BATCH = 1

        def _group_norm(y, weight, bias):
            g = y.reshape(y.shape[:-1] + (GROUPS, -1))
            mean = g.mean(axis=-1, keepdims=True)
            var = g.var(axis=-1, keepdims=True)
            g = (g - mean) * jax.lax.rsqrt(var + EPS)
            return g.reshape(y.shape) * weight + bias

        def gate_loop_operator(k, v, q, a):
            kv = (k[..., :, None] * v[..., None, :]).astype(a.dtype)
            aa = a[..., :, None]

            def binop(e_i, e_j):
                a_i, kv_i = e_i
                a_j, kv_j = e_j
                return (a_j * a_i, a_j * kv_i + kv_j)
            _, y = jax.lax.associative_scan(binop, (aa, kv), axis=1)
            y = jnp.real(y).astype(k.dtype)
            return jnp.einsum('bld,blde->ble', q, y)
        q = x @ wq
        k = x @ wk
        v = x @ wv
        g = x @ wg
        a = (x @ wa).astype(jnp.float32)
        a_real, a_imag = jnp.split(a, 2, axis=-1)
        a_complex = jax.nn.sigmoid(a_real) * jnp.exp(1j * a_imag)
        y = gate_loop_operator(k, v, q, a_complex)
        y = _group_norm(y, gn_weight, gn_bias)
        y = y * jax.nn.silu(g)
        return y @ wo + bias

    def _L0_ffn_ref(x, attention_mask, wr, br, w1, b1, w2, b2):
        import jax, jax.numpy as jnp
        import numpy as np
        B, S, D = (8, 1024, 64)
        H = 4 * D
        CAPACITY = 0.5
        b, s, d = x.shape
        weights = (jnp.einsum('bsd,do->bso', x, wr) + br)[..., 0]
        k = max(1, int(CAPACITY * s))
        kk = k - 1 if k > 1 else 1
        _, idx = jax.lax.top_k(weights, k)
        sel_idx = idx[:, :kk]
        sel = jnp.take_along_axis(x, sel_idx[:, :, None], axis=1)
        h = jax.nn.gelu(jnp.einsum('bkd,dh->bkh', sel, w1) + b1)
        y = jnp.einsum('bkh,hd->bkd', h, w2) + b2
        w_sel = jnp.take_along_axis(weights, sel_idx, axis=1)
        y = y * w_sel[..., None]
        batch_idx = jnp.arange(b)[:, None]
        processed = jnp.zeros_like(x).at[batch_idx, sel_idx].set(y)
        return processed + x

    def _L1_attn_ref(x_in, W_ih, W_hh, b_ih, b_hh):
        import jax, jax.numpy as jnp
        import numpy as np
        SEQ, BATCH, IN, HID = (512, 64, 64, 64)
        xp = jnp.einsum('tbi,hi->tbh', x_in, W_ih) + b_ih + b_hh
        h0 = jnp.zeros((x_in.shape[1], W_hh.shape[0]), dtype=x_in.dtype)

        def step(h, xp_t):
            h_new = jnp.tanh(xp_t + h @ W_hh.T)
            return (h_new, h_new)
        _, hiddens = jax.lax.scan(step, h0, xp)
        return hiddens

    def _L1_ffn_ref(x, ln1_w, ln2_w, wq, wk, wv, wo, router_w, w1, w2, w3):
        import jax, jax.numpy as jnp
        import numpy as np
        B, T, C = (64, 96, 64)
        NH, NKV = (4, 2)
        HD = C // NH
        NREP = NH // NKV
        NE, TOPK = (8, 2)
        HID = int(8 / 3 * C)
        EPS_RMS = 1e-06

        def _rope_tables(t_len):
            inv_freq = 1.0 / 10000.0 ** (np.arange(0, HD, 2, dtype=np.float32) / HD)
            t = np.arange(t_len, dtype=np.float32)
            freqs = np.outer(t, inv_freq)
            emb = np.concatenate([freqs, freqs], axis=-1)
            return (jnp.asarray(np.cos(emb)), jnp.asarray(np.sin(emb)))

        def _rotate_half(x):
            h = x.shape[-1] // 2
            return jnp.concatenate([-x[..., h:], x[..., :h]], axis=-1)

        def _rmsnorm(v, w):
            return v * jax.lax.rsqrt(jnp.mean(v * v, axis=-1, keepdims=True) + EPS_RMS) * w
        Bx, Tx, Cx = x.shape
        h = _rmsnorm(x, ln1_w)
        q = (h @ wq.T).reshape(Bx, Tx, NH, HD).transpose(0, 2, 1, 3)
        k = (h @ wk.T).reshape(Bx, Tx, NKV, HD).transpose(0, 2, 1, 3)
        v = (h @ wv.T).reshape(Bx, Tx, NKV, HD).transpose(0, 2, 1, 3)
        cos, sin = _rope_tables(Tx)
        cos, sin = (cos[None, None], sin[None, None])
        q = q * cos + _rotate_half(q) * sin
        k = k * cos + _rotate_half(k) * sin
        k = jnp.repeat(k, NREP, axis=1)
        v = jnp.repeat(v, NREP, axis=1)
        scores = jnp.einsum('bhtd,bhsd->bhts', q, k) / jnp.sqrt(jnp.float32(HD))
        causal = jnp.tril(jnp.ones((Tx, Tx), dtype=bool))
        scores = jnp.where(causal[None, None], scores, jnp.float32(-1e+30))
        att = jax.nn.softmax(scores, axis=-1)
        y = jnp.einsum('bhts,bhsd->bhtd', att, v).transpose(0, 2, 1, 3).reshape(Bx, Tx, Cx)
        x = x + y @ wo.T
        flat = _rmsnorm(x, ln2_w).reshape(-1, Cx)
        probs = jax.nn.softmax(flat @ router_w.T, axis=-1)
        tp, ti = jax.lax.top_k(probs, TOPK)
        tp = tp / (jnp.sum(tp, axis=-1, keepdims=True) + 1e-09)
        weights = jnp.sum(tp[..., None] * jax.nn.one_hot(ti, NE, dtype=flat.dtype), axis=1)
        out = jnp.zeros_like(flat)
        for e in range(NE):
            hh = jax.nn.silu(flat @ w1[e].T) * (flat @ w3[e].T)
            out = out + weights[:, e:e + 1] * (hh @ w2[e].T)
        return x + out.reshape(Bx, Tx, Cx)
    h = _L0_tok_ref(x, L0_tok_W, L0_tok_b, L0_tok_pos)
    h = jnp.concatenate([jnp.broadcast_to(cls_tok, (h.shape[0], 1, h.shape[2])), h], axis=1)
    h = h + _L0_attn_ref(_layernorm(h, axis=-1), L0_attn_wq, L0_attn_wk, L0_attn_wv, L0_attn_wa, L0_attn_wg, L0_attn_wo, L0_attn_gn_weight, L0_attn_gn_bias, L0_attn_bias)
    h = h + _L0_ffn_ref(_layernorm(h, axis=-1), L0_ffn_attention_mask, L0_ffn_wr, L0_ffn_br, L0_ffn_w1, L0_ffn_b1, L0_ffn_w2, L0_ffn_b2)
    h = h + _L1_attn_ref(_layernorm(h, axis=-1), L1_attn_W_ih, L1_attn_W_hh, L1_attn_b_ih, L1_attn_b_hh)
    h = h + _L1_ffn_ref(_layernorm(h, axis=-1), L1_ffn_ln1_w, L1_ffn_ln2_w, L1_ffn_wq, L1_ffn_wk, L1_ffn_wv, L1_ffn_wo, L1_ffn_router_w, L1_ffn_w1, L1_ffn_w2, L1_ffn_w3)
    return h

_drawn_inputs = setup_inputs


def setup_inputs(seed=0):
    import zlib

    import numpy as np

    out = dict(_drawn_inputs(seed))
    spreads = {'L0_attn_gn_weight': (1.0, 0.2),
     'L0_attn_gn_bias': (0.0, 0.1),
     'L0_attn_bias': (0.0, 0.1),
     'L0_ffn_b1': (0.0, 0.8),
     'L0_ffn_b2': (0.0, 0.8),
     'L1_ffn_ln1_w': (1.0, 0.6),
     'L1_ffn_ln2_w': (1.0, 0.6)}
    factors = {'cls_tok': 4.636,
     'L0_ffn_wr': 8.0,
     'L0_ffn_w1': 8.0,
     'L0_ffn_w2': 8.0,
     'L1_ffn_wq': 8.0,
     'L1_ffn_wk': 8.0,
     'L1_ffn_wv': 8.0,
     'L1_ffn_wo': 8.0,
     'L1_ffn_router_w': 8.0,
     'L1_ffn_w1': 8.0,
     'L1_ffn_w2': 8.0,
     'L1_ffn_w3': 8.0}
    for name, (base, spread) in spreads.items():
        noise = np.random.default_rng([zlib.crc32(name.encode()), seed]).standard_normal(out[name].shape)
        drawn = base * np.exp(spread * noise) if base else spread * noise
        out[name] = jnp.asarray(drawn.astype(out[name].dtype))
    for name, factor in factors.items():
        out[name] = (out[name] * factor).astype(out[name].dtype)
    return out
```

```python
import numpy as np
import concourse.bass as bass
from concourse import mybir
from contextlib import ExitStack

F32 = mybir.dt.float32
BF16 = mybir.dt.bfloat16
ALU = mybir.AluOpType
ACT = mybir.ActivationFunctionType
AX = mybir.AxisListType

B = 32
D = 64
T = 1025
CH = 257
HP = 2 * CH
TP = 2 * HP
PD = 49
KSEL = 511
NH, NKV, HD = 4, 2, 16
TB, NTB = 114, 9
SB, NSB = 128, 8
TC, NTC = 342, 3
TQ = TC * NTC
NE, HID = 8, 170
NTL = -(-NE * HID // 128)
RB = 103
NEG = -1.0e30
LOWEST = -3.4028234663852886e38
HUGE = 3.0e38
TERMS = [(0, 0), (0, 1), (1, 0), (1, 1), (0, 2), (2, 0)]
NT = len(TERMS)


class Place:

    def __init__(self, nc):
        self.nc = nc
        self.sems = ExitStack()
        self.used = []

    def sb(self, ctx, name, shape, dt=F32):
        return ctx.enter_context(self.nc.sbuf_tensor(name, shape, dt))

    def ps(self, ctx, name, shape, dt=F32):
        return ctx.enter_context(self.nc.psum_tensor(name, shape, dt))

    def sem(self, name):
        self.used.append(self.sems.enter_context(self.nc.semaphore(name)))
        return self.used[-1]

    def clear(self):
        used, self.used = self.used, []
        with self.nc.Block() as block:
            @block.sync
            def _(sp):
                for s in used:
                    sp.sem_clear(s)
        self.sems.close()


def wait_alone(eng, sem, value, passed):
    eng.wait_ge(sem, value)
    eng.sem_inc(passed, 1)


def mm2(nc, out, lhsT, rhs, start=True, stop=True):
    for c in range(2):
        last = nc.tensor.matmul(out[:, c, 0:CH], lhsT, rhs[:, c, :], start=start, stop=stop)
    return last


def cut(nc, step, dve, src, p1, rest, p2, p3, n):
    for ins in (lambda: nc.vector.tensor_copy(p1, src),
                lambda: nc.vector.tensor_tensor(rest, src, p1, ALU.subtract),
                lambda: nc.vector.tensor_copy(p2, rest),
                lambda: nc.vector.tensor_tensor(p3, rest, p2, ALU.subtract)):
        ins().then_inc(step, 1)
        n += 1
        dve.wait_ge(step, n)
    return n


def load_phase(nc, P, dmas, name):
    ready = P.sem(f"{name}_consts")
    with nc.Block() as block:
        @block.sync
        def _(sp):
            for dst, src in dmas:
                sp.dma_start(dst, src).then_inc(ready, 16)
            sp.wait_ge(ready, 16 * len(dmas))


def embed_phase(nc, P, A, H):
    with ExitStack() as c:
        wtok = P.sb(c, "wtok", [2 * PD, 128])
        pos = P.sb(c, "pos", [128, HP])
        tokb = P.sb(c, "tokb", [128, 1])
        patch = [P.sb(c, f"patch{k}", [2 * PD, 2, CH]) for k in range(2)]
        emb = [P.ps(c, f"emb{k}", [128, 2, 512]) for k in range(2)]
        load_phase(nc, P, [(wtok[:], A["wtok"]), (pos[:], A["pos"]), (tokb[:], A["tokb"])], "embed")
        posb_ready, patch_free = P.sem("posb_ready"), P.sem("patch_free")
        patch_ready = [P.sem(f"patch_ready{k}") for k in range(2)]
        emb_ready, emb_free = P.sem("emb_ready"), P.sem("emb_free")
        patches = A["patches"].rearrange("p (b c n) -> p b c n", b=B, c=2)
        with nc.Block() as block:
            @block.sync
            def _(sp):
                with sp.Fori(0, B // 2) as j:
                    for k in range(2):
                        i = 2 * j + k
                        sp.wait_ge(patch_free, i + 1)
                        sp.dma_start(patch[k][:], patches[:, i, :, :]).then_inc(patch_ready[k], 16)

            @block.tensor
            def _(pe):
                pe.sem_inc(patch_free, 2)
                with pe.Fori(0, B // 2) as j:
                    for k in range(2):
                        i = 2 * j + k
                        pe.wait_ge(patch_ready[k], 16 * j + 16)
                        pe.wait_ge(emb_free, i + 1)
                        last = mm2(nc, emb[k], wtok[:], patch[k])
                        last.then_inc(emb_ready, 1)
                        pe.wait_ge(emb_ready, i + 1)
                        pe.sem_inc(patch_free, 1)

            @block.vector
            def _(dve):
                nc.vector.tensor_scalar(pos[0:64, 1:HP], pos[0:64, 1:HP], tokb[0:64, 0:1], None, ALU.add)
                nc.vector.tensor_scalar(pos[64:128, :], pos[64:128, :], tokb[64:128, 0:1], None,
                                        ALU.add).then_inc(posb_ready, 1)
                dve.wait_ge(posb_ready, 1)
                dve.sem_inc(emb_free, 2)
                pos2 = pos[:].rearrange("p (c n) -> p c n", c=2)
                with dve.Fori(0, B // 2) as j:
                    for k in range(2):
                        i = 2 * j + k
                        dve.wait_ge(emb_ready, i + 1)
                        nc.vector.tensor_tensor(H[:, i, :, :], emb[k][:, :, 0:CH], pos2,
                                                ALU.add).then_inc(emb_free, 1)


def norm_phase(nc, P, name, cst, src, dst, eps, centre, spill=None):
    with ExitStack() as c:
        sq = [P.sb(c, f"{name}_sq{k}", [128, 2, CH]) for k in range(2)]
        lg = [P.sb(c, f"{name}_lg{k}", [128, 2, CH]) for k in range(2)]
        rs = [P.sb(c, f"{name}_rs{k}", [128, 2, CH]) for k in range(2)]
        cen = [P.ps(c, f"{name}_cen{k}", [128, 2, 512]) for k in range(2)]
        var = [P.ps(c, f"{name}_var{k}", [128, 2, 512]) for k in range(2)]
        centred, squared, var_ready = (P.sem(f"{name}_{x}") for x in ("centred", "squared", "var_ready"))
        var_read, rstd_ready, normed = (P.sem(f"{name}_{x}") for x in ("var_read", "rstd_ready", "normed"))
        spilled = P.sem(f"{name}_spilled")
        with nc.Block() as block:
            if spill is not None:
                @block.sync
                def _(sp):
                    sp.dma_start(spill, src[:].rearrange("p b c n -> p (b c n)")).then_inc(spilled, 16)
                    sp.wait_ge(spilled, 16)

            @block.tensor
            def _(pe):
                with pe.Fori(0, B // 2) as j:
                    if centre:
                        for k in range(2):
                            i = 2 * j + k
                            pe.wait_ge(normed, i + 1)
                            mm2(nc, cen[k], cst["centre"], src[:, i, :, :]).then_inc(centred, 1)
                    for k in range(2):
                        i = 2 * j + k
                        pe.wait_ge(squared, i + 1)
                        pe.wait_ge(var_read, i + 1)
                        mm2(nc, var[k], cst["average"], sq[k]).then_inc(var_ready, 1)

            @block.scalar
            def _(act):
                act.preload_act_table_set("natural_log_exp_and_others")
                act.sem_inc(var_read, 2)
                with act.Fori(0, B // 2) as j:
                    for k in range(2):
                        i = 2 * j + k
                        if centre:
                            act.wait_ge(centred, i + 1)
                            nc.scalar.activation(sq[k][:], cen[k][:, :, 0:CH], ACT.Square).then_inc(squared, 1)
                        else:
                            nc.scalar.activation(sq[k][:], src[:, i, :, :], ACT.Square).then_inc(squared, 1)
                    for k in range(2):
                        i = 2 * j + k
                        act.wait_ge(var_ready, i + 1)
                        nc.scalar.activation(lg[k][:], var[k][:, :, 0:CH], ACT.Ln, bias=eps).then_inc(var_read, 1)
                    for k in range(2):
                        i = 2 * j + k
                        act.wait_ge(var_read, i + 3)
                        act.wait_ge(normed, i + 1)
                        nc.scalar.activation(rs[k][:], lg[k][:], ACT.Exp, scale=-0.5).then_inc(rstd_ready, 1)

            @block.vector
            def _(dve):
                dve.sem_inc(normed, 2)
                with dve.Fori(0, B // 2) as j:
                    for k in range(2):
                        i = 2 * j + k
                        dve.wait_ge(rstd_ready, i + 1)
                        left = cen[k][:, :, 0:CH] if centre else src[:, i, :, :]
                        nc.vector.tensor_tensor(dst[:, i, :, :], left, rs[k][:], ALU.mult).then_inc(normed, 1)


def gate_phase(nc, P, A, H, XN):
    with ExitStack() as c:
        wg, wo = P.sb(c, "gate_wg", [128, 128]), P.sb(c, "gate_wo", [128, 128])
        gnb, ab = P.sb(c, "gate_gnb", [128, 1]), P.sb(c, "gate_ab", [128, 1])
        sl = [P.sb(c, f"gate_sl{k}", [128, 2, CH]) for k in range(2)]
        g = [P.ps(c, f"gate_g{k}", [128, 2, 512]) for k in range(2)]
        y = [P.ps(c, f"gate_y{k}", [128, 2, 512]) for k in range(2)]
        load_phase(nc, P, [(wg[:], A["wg"]), (wo[:], A["wo"]), (gnb[:], A["gnb"]), (ab[:], A["attn_b"])], "gate")
        wo_scaled, g_ready, silu_ready = (P.sem(f"gate_{x}") for x in ("wo_scaled", "g_ready", "silu_ready"))
        y_ready, y_added = P.sem("gate_y_ready"), P.sem("gate_y_added")
        with nc.Block() as block:
            @block.tensor
            def _(pe):
                pe.wait_ge(wo_scaled, 1)
                with pe.Fori(0, B // 2) as j:
                    for k in range(2):
                        i = 2 * j + k
                        pe.wait_ge(y_added, i + 1)
                        mm2(nc, g[k], wg[:], XN[:, i, :, :]).then_inc(g_ready, 1)
                    for k in range(2):
                        i = 2 * j + k
                        pe.wait_ge(silu_ready, i + 1)
                        mm2(nc, y[k], wo[:], sl[k]).then_inc(y_ready, 1)

            @block.scalar
            def _(act):
                act.preload_act_table_set("silu_and_others")
                with act.Fori(0, B // 2) as j:
                    for k in range(2):
                        i = 2 * j + k
                        act.wait_ge(g_ready, i + 1)
                        nc.scalar.activation(sl[k][:], g[k][:, :, 0:CH], ACT.Silu).then_inc(silu_ready, 1)

            @block.vector
            def _(dve):
                nc.vector.tensor_scalar(wo[:], wo[:], gnb[:, 0:1], None, ALU.mult).then_inc(wo_scaled, 1)
                dve.sem_inc(y_added, 2)
                with dve.Fori(0, B // 2) as j:
                    for k in range(2):
                        i = 2 * j + k
                        dve.wait_ge(y_ready, i + 1)
                        nc.vector.scalar_tensor_tensor(H[:, i, :, :], y[k][:, :, 0:CH], ab[:, 0:1], H[:, i, :, :],
                                                       ALU.add, ALU.add).then_inc(y_added, 1)


def token_weight_phase(nc, P, A, XN, wr_rows):
    with ExitStack() as c:
        wr, br = P.sb(c, "wr", [128, 128]), P.sb(c, "br", [128, 1])
        row = [P.sb(c, f"wr_row{k}", [128, 2, CH]) for k in range(2)]
        w = [P.ps(c, f"wr_ps{k}", [128, 2, 512]) for k in range(2)]
        load_phase(nc, P, [(wr[:], A["wr"]), (br[:], A["br"])], "wr")
        w_ready, w_copied = P.sem("wr_ready"), P.sem("wr_copied")
        stored = [P.sem(f"wr_stored{k}") for k in range(2)]
        with nc.Block() as block:
            @block.tensor
            def _(pe):
                with pe.Fori(0, B // 2) as j:
                    for k in range(2):
                        i = 2 * j + k
                        pe.wait_ge(w_copied, i + 1)
                        mm2(nc, w[k], wr[:], XN[:, i, :, :]).then_inc(w_ready, 1)

            @block.scalar
            def _(act):
                act.sem_inc(w_copied, 2)
                for k in range(2):
                    act.sem_inc(stored[k], 32)
                with act.Fori(0, B // 2) as j:
                    for k in range(2):
                        i = 2 * j + k
                        act.wait_ge(w_ready, i + 1)
                        act.wait_ge(stored[k], 32 * j + 32)
                        nc.scalar.activation(row[k][:], w[k][:, :, 0:CH], ACT.Identity,
                                             bias=br[:, 0:1]).then_inc(w_copied, 1)

            @block.sync
            def _(sp):
                with sp.Fori(0, B // 2) as j:
                    for k in range(2):
                        i = 2 * j + k
                        sp.wait_ge(w_copied, i + 3)
                        for h in range(2):
                            sp.dma_start(wr_rows[bass.ds(i, 1), h, :],
                                         row[k][64 * h:64 * h + 1, :, :].rearrange("p c n -> p (c n)"))\
                                .then_inc(stored[k], 16)
                for k in range(2):
                    sp.wait_ge(stored[k], 32 * (B // 2) + 32)


def top_phase(nc, P, wr_rows, sel_rows):
    with ExitStack() as c:
        w = P.sb(c, "top_w", [B, TP])
        left = P.sb(c, "top_left", [B, T + 1])
        most = P.sb(c, "top_most", [B, 8])
        loaded, step, stored = P.sem("top_loaded"), P.sem("top_step"), P.sem("top_stored")
        passed = P.sem("top_passed")
        with nc.Block() as block:
            @block.sync
            def _(sp):
                sp.dma_start(w[:], wr_rows.rearrange("b h n -> b (h n)")).then_inc(loaded, 16)
                sp.wait_ge(step, 2 + 128 + 3)
                sp.dma_start(sel_rows.rearrange("b h n -> b (h n)"), w[:]).then_inc(stored, 16)
                sp.wait_ge(stored, 16)

            @block.vector
            def _(dve):
                dve.wait_ge(loaded, 16)
                nc.vector.memset(left[:, T:T + 1], HUGE).then_inc(step, 1)
                nc.vector.tensor_copy(left[:, 0:T], w[:, 0:T]).then_inc(step, 1)
                with dve.Fori(0, (KSEL + 1) // 8) as r:
                    wait_alone(dve, step, 2 * r + 2, passed)
                    nc.vector.max(most[:], left[:]).then_inc(step, 1)
                    wait_alone(dve, step, 2 * r + 3, passed)
                    nc.vector.match_replace(left[:], most[:], left[:], LOWEST).then_inc(step, 1)
                dve.wait_ge(step, 130)
                nc.vector.tensor_tensor(left[:, 0:T], left[:, 0:T], w[:, 0:T], ALU.not_equal).then_inc(step, 1)
                dve.wait_ge(step, 131)
                nc.vector.tensor_tensor(w[:, 0:T], left[:, 0:T], w[:, 0:T], ALU.mult).then_inc(step, 1)
                nc.vector.memset(w[:, T:TP], 0.0).then_inc(step, 1)


def mlp_phase(nc, P, A, H, XN, sel_rows):
    with ExitStack() as c:
        w1, w2 = P.sb(c, "mlp_w1", [128, 4, 128]), P.sb(c, "mlp_w2", [128, 4, 128])
        b1, b2 = P.sb(c, "mlp_b1", [128, 4]), P.sb(c, "mlp_b2", [128, 1])
        act_out = [P.sb(c, f"mlp_g{k}", [128, 4, 2, CH]) for k in range(2)]
        sel = [P.sb(c, f"mlp_sel{k}", [128, 2, CH]) for k in range(2)]
        tmp = [P.sb(c, f"mlp_t{k}", [128, 2, CH]) for k in range(2)]
        u = [P.ps(c, f"mlp_u{k}", [128, 2, 512]) for k in range(2)]
        y = [P.ps(c, f"mlp_y{k}", [128, 2, 512]) for k in range(2)]
        load_phase(nc, P, [(w1[:], A["w1"]), (w2[:], A["w2"]), (b1[:], A["b1"]), (b2[:], A["b2"])], "mlp")
        u_ready, gelu_ready, y_ready, y_read = (P.sem(f"mlp_{x}") for x in ("u_ready", "gelu_ready", "y_ready", "y_read"))
        t_ready, r_ready = P.sem("mlp_t_ready"), P.sem("mlp_r_ready")
        sel_ready = [P.sem(f"mlp_sel_ready{k}") for k in range(2)]
        with nc.Block() as block:
            @block.sync
            def _(sp):
                with sp.Fori(0, B // 2) as j:
                    for k in range(2):
                        i = 2 * j + k
                        sp.wait_ge(y_read, i + 1)
                        for h in range(2):
                            sp.dma_start(sel[k][64 * h:64 * h + 64, :, :].rearrange("p c n -> p (c n)"),
                                         sel_rows[bass.ds(i, 1), h, :].broadcast_to([64, HP]))\
                                .then_inc(sel_ready[k], 16)

            @block.tensor
            def _(pe):
                with pe.Fori(0, B // 2) as j:
                    for k in range(2):
                        i = 2 * j + k
                        for m in range(4):
                            pe.wait_ge(gelu_ready, 4 * i + m + 1)
                            mm2(nc, u[m % 2], w1[:, m, :], XN[:, i, :, :]).then_inc(u_ready, 1)
                    for k in range(2):
                        i = 2 * j + k
                        pe.wait_ge(gelu_ready, 4 * i + 6)
                        pe.wait_ge(y_read, i + 1)
                        for m in range(4):
                            last = mm2(nc, y[k], w2[:, m, :], act_out[k][:, m, :, :], m == 0, m == 3)
                        last.then_inc(y_ready, 1)

            @block.scalar
            def _(act):
                act.preload_act_table_set("gelu_apprx_tanh_and_others")
                act.sem_inc(gelu_ready, 2)
                with act.Fori(0, B // 2) as j:
                    for k in range(2):
                        i = 2 * j + k
                        for m in range(4):
                            act.wait_ge(u_ready, 4 * i + m + 1)
                            nc.scalar.activation(act_out[k][:, m, :, :], u[m % 2][:, :, 0:CH], ACT.Gelu_apprx_tanh,
                                                 bias=b1[:, m:m + 1]).then_inc(gelu_ready, 1)

            @block.gpsimd
            def _(pool):
                with pool.Fori(0, B // 2) as j:
                    for k in range(2):
                        i = 2 * j + k
                        nc.gpsimd.tensor_tensor(H[:, i, :, :], H[:, i, :, :], XN[:, i, :, :], op=ALU.add)\
                            .then_inc(r_ready, 1)

            @block.vector
            def _(dve):
                dve.sem_inc(y_read, 2)
                dve.sem_inc(t_ready, 2)
                with dve.Fori(0, B // 2) as j:
                    for k in range(2):
                        i = 2 * j + k
                        dve.wait_ge(y_ready, i + 1)
                        dve.wait_ge(sel_ready[k], 32 * j + 32)
                        dve.wait_ge(t_ready, i + 1)
                        nc.vector.scalar_tensor_tensor(tmp[k][:], y[k][:, :, 0:CH], b2[:, 0:1], sel[k][:],
                                                       ALU.add, ALU.mult).then_inc(y_read, 1)
                    for k in range(2):
                        i = 2 * j + k
                        dve.wait_ge(y_read, i + 3)
                        dve.wait_ge(r_ready, i + 1)
                        nc.vector.tensor_tensor(H[:, i, :, :], H[:, i, :, :], tmp[k][:], ALU.add).then_inc(t_ready, 1)
                dve.wait_ge(t_ready, B + 2)


def rnn_phase(nc, P, A, H, XN):
    with ExitStack() as c:
        wih, whh = P.sb(c, "wih", [128, 128]), P.sb(c, "whh", [128, 128])
        bih, bhh = P.sb(c, "bih", [128, 1]), P.sb(c, "bhh", [128, 1])
        hid = [P.sb(c, f"hid{k}", [128, 2, CH]) for k in range(2)]
        z = [P.ps(c, f"rnn_z{k}", [128, 2, 512]) for k in range(2)]
        load_phase(nc, P, [(wih[:], A["wih"]), (whh[:], A["whh"]), (bih[:], A["bih"]), (bhh[:], A["bhh"])], "rnn")
        bias_ready, z_ready = P.sem("rnn_bias_ready"), [P.sem(f"rnn_z_ready{q}") for q in range(2)]
        tanh_done, added = [P.sem(f"rnn_tanh{q}") for q in range(2)], P.sem("rnn_added")
        with nc.Block() as block:
            @block.tensor
            def _(pe):
                with pe.Fori(0, B // 2) as j:
                    for k in range(2):
                        i = 2 * j + k
                        for q in range(2):
                            nc.tensor.matmul(z[k][:, q, 0:CH], wih[:], XN[:, i, q, :], start=True, stop=False)
                        for q in range(2):
                            pe.wait_ge(tanh_done[q], i + 1)
                            nc.tensor.matmul(z[k][:, q, 0:CH], whh[:], hid[1 - k][:, q, :], start=False, stop=True)\
                                .then_inc(z_ready[q], 1)

            @block.scalar
            def _(act):
                act.preload_act_table_set("exp_and_others")
                act.wait_ge(bias_ready, 1)
                with act.Fori(0, B // 2) as j:
                    for k in range(2):
                        i = 2 * j + k
                        for q in range(2):
                            act.wait_ge(z_ready[q], i + 1)
                            act.wait_ge(added, i + 1)
                            nc.scalar.activation(hid[k][:, q, :], z[k][:, q, 0:CH], ACT.Tanh, bias=bih[:, 0:1])\
                                .then_inc(tanh_done[q], 1)

            @block.vector
            def _(dve):
                nc.vector.tensor_tensor(bih[:], bih[:], bhh[:], ALU.add).then_inc(bias_ready, 1)
                for q in range(2):
                    nc.vector.memset(hid[1][:, q, :], 0.0).then_inc(tanh_done[q], 1)
                dve.sem_inc(added, 2)
                with dve.Fori(0, B // 2) as j:
                    for k in range(2):
                        i = 2 * j + k
                        for q in range(2):
                            dve.wait_ge(tanh_done[q], i + 2)
                        nc.vector.tensor_tensor(H[:, i, :, :], H[:, i, :, :], hid[k][:], ALU.add).then_inc(added, 1)


def qkv_phase(nc, P, A, HN, cst, parts_d, va_d):
    NQK = (NH + NKV) * HD
    with ExitStack() as c:
        wq = P.sb(c, "wqkv", [128, 2, 2, 128])
        ln1 = P.sb(c, "ln1", [128, 1])
        cos, sin = P.sb(c, "cos", [NQK, TP]), P.sb(c, "sin", [NQK, TP])
        qc = [P.sb(c, f"qc{k}", [NQK, TP]) for k in range(2)]
        qs = [P.sb(c, f"qs{k}", [NQK, TP]) for k in range(2)]
        r1 = [P.sb(c, f"r1_{k}", [NQK, TP]) for k in range(2)]
        part = [P.sb(c, f"part{k}", [NQK, 3, TP], BF16) for k in range(2)]
        vt = [P.sb(c, f"vt{k}", [128, TP]) for k in range(2)]
        va = [P.sb(c, f"va{k}", [128, NTB, NH, 32]) for k in range(2)]
        plain = [P.ps(c, f"plain{h}", [128, 2, 512]) for h in range(2)]
        turned = [P.ps(c, f"turned{h}", [128, 512]) for h in range(2)]
        vtp = [P.ps(c, f"vtp{h}", [128, 512]) for h in range(2)]
        load_phase(nc, P, [(wq[:].rearrange("p a b m -> p (a b m)"), A["wqkv"]), (ln1[:], A["ln1"]),
                           (cos[:], A["cos"]), (sin[:], A["sin"])], "qkv")
        w_scaled, ones_set = P.sem("qkv_w_scaled"), P.sem("va_ones")
        plain_ready, turned_ready = P.sem("plain_ready"), P.sem("turned_ready")
        cos_done, sin_done, v_copied = P.sem("cos_done"), P.sem("sin_done"), P.sem("v_copied")
        sum_done, p1_done, d1_done, p2_done, p3_done = (P.sem(x) for x in ("qk_sum", "part1", "rest1", "part2", "part3"))
        v_turned, va_done = P.sem("v_turned"), P.sem("va_done")
        stored = [P.sem(f"qkv_stored{k}") for k in range(2)]
        passed = P.sem("qkv_passed")
        with nc.Block() as block:
            @block.vector
            def _(dve):
                nc.vector.tensor_scalar(wq[:], wq[:], ln1[:, 0:1], None, ALU.mult).then_inc(w_scaled, 1)
                for k in range(2):
                    nc.vector.memset(va[k][:, :, :, HD:32], 1.0).then_inc(ones_set, 1)
                    nc.vector.memset(va[k][:, NTB - 1, :, 0:HD], 0.0).then_inc(ones_set, 1)
                dve.wait_ge(ones_set, 4)
                dve.sem_inc(cos_done, 2)
                dve.sem_inc(sin_done, 2)
                dve.sem_inc(va_done, 2)
                with dve.Fori(0, B // 2) as j:
                    for k in range(2):
                        i = 2 * j + k
                        for h in range(2):
                            for q in range(2):
                                s = slice(HP * h + CH * q, HP * h + CH * q + CH)
                                if q == 0:
                                    dve.wait_ge(plain_ready, 2 * i + h + 1)
                                    if h == 0:
                                        dve.wait_ge(p3_done, i + 1)
                                    last = nc.vector.tensor_tensor(
                                        qc[k][:, HP * h:HP * h + HP].rearrange("p (c n) -> p c n", c=2),
                                        plain[h][0:NQK, :, 0:CH],
                                        cos[:, HP * h:HP * h + HP].rearrange("p (c n) -> p c n", c=2), ALU.mult)
                                    last.then_inc(cos_done, 1)
                                dve.wait_ge(turned_ready, 4 * i + 2 * h + q + 1)
                                nc.vector.tensor_tensor(qs[k][:, s], turned[q][0:NQK, 0:CH], sin[:, s],
                                                        ALU.mult).then_inc(sin_done, 1)
                        dve.wait_ge(v_turned, i + 1)
                        dve.wait_ge(stored[k], 64 * j + 64)
                        vv = vtp[k][:, 0:NSB * 32].rearrange("p (b g d) -> p b g d", b=NSB, g=NKV)
                        for r in range(2):
                            nc.vector.tensor_copy(
                                va[k][:, 0:NSB, r:NH:2, 0:HD], vv)
                            last = nc.vector.tensor_copy(
                                va[k][0:4, NSB, r:NH:2, 0:HD],
                                vtp[k][0:4, NSB * 32:NTB * 32].rearrange("p (g d) -> p g d", g=NKV))
                        last.then_inc(va_done, 1)
                        dve.wait_ge(cos_done, 2 * i + 4)
                        dve.wait_ge(sin_done, 4 * i + 6)
                        nc.vector.tensor_tensor(qc[k][:], qc[k][:], qs[k][:], ALU.add).then_inc(sum_done, 1)
                        dve.wait_ge(p2_done, i + 1)
                        nc.vector.tensor_tensor(part[k][:, 2, :], r1[k][:], part[k][:, 1, :],
                                                ALU.subtract).then_inc(p3_done, 1)

            @block.tensor
            def _(pe):
                pe.wait_ge(w_scaled, 1)
                with pe.Fori(0, B // 2) as j:
                    for k in range(2):
                        i = 2 * j + k
                        for h in range(2):
                            pe.wait_ge(cos_done, 2 * i + h + 1)
                            pe.wait_ge(v_copied, 2 * i + h + 1)
                            mm2(nc, plain[h], wq[:, h, 0, :], HN[:, i, :, :]).then_inc(plain_ready, 1)
                            for q in range(2):
                                pe.wait_ge(sin_done, 4 * i + 2 * h + q + 1)
                                nc.tensor.matmul(turned[q][0:NQK, 0:CH], wq[:, h, 1, 0:NQK], HN[:, i, q, :],
                                                 start=True, stop=True).then_inc(turned_ready, 1)
                        pe.wait_ge(v_copied, 2 * i + 4)
                        wait_alone(pe, va_done, i + 1, passed)
                        for b in range(NTB):
                            n = min(128, TP - 128 * b)
                            last = nc.tensor.transpose(vtp[k][0:n, 32 * b:32 * b + 32],
                                                       vt[k][96:128, 128 * b:128 * b + n],
                                                       cst["ident"][96:128, 96:128])
                        last.then_inc(v_turned, 1)

            @block.scalar
            def _(act):
                act.sem_inc(v_copied, 2)
                with act.Fori(0, B // 2) as j:
                    for k in range(2):
                        i = 2 * j + k
                        for h in range(2):
                            act.wait_ge(plain_ready, 2 * i + h + 1)
                            act.wait_ge(va_done, i + 1)
                            nc.scalar.activation(
                                vt[k][96:128, HP * h:HP * h + HP].rearrange("p (c n) -> p c n", c=2),
                                plain[h][96:128, :, 0:CH], ACT.Copy).then_inc(v_copied, 1)
                        act.wait_ge(sum_done, i + 1)
                        act.wait_ge(stored[k], 64 * j + 64)
                        nc.scalar.activation(part[k][:, 0, :], qc[k][:], ACT.Copy).then_inc(p1_done, 1)
                        act.wait_ge(d1_done, i + 3)
                        nc.scalar.activation(part[k][:, 1, :], r1[k][:], ACT.Copy).then_inc(p2_done, 1)

            @block.gpsimd
            def _(pool):
                pool.sem_inc(d1_done, 2)
                pool.sem_inc(p3_done, 2)
                with pool.Fori(0, B // 2) as j:
                    for k in range(2):
                        i = 2 * j + k
                        pool.wait_ge(p1_done, i + 1)
                        pool.wait_ge(p3_done, i + 1)
                        nc.gpsimd.tensor_tensor(r1[k][:], qc[k][:], part[k][:, 0, :], op=ALU.subtract)\
                            .then_inc(d1_done, 1)

            @block.sync
            def _(sp):
                for k in range(2):
                    sp.sem_inc(stored[k], 64)
                with sp.Fori(0, B // 2) as j:
                    for k in range(2):
                        i = 2 * j + k
                        sp.wait_ge(va_done, i + 3)
                        sp.dma_start(va_d[bass.ds(i, 1), :, :].rearrange("a p n -> (a p) n"),
                                     va[k][:].rearrange("p b h d -> p (b h d)")).then_inc(stored[k], 16)
                        for m, done in enumerate((p1_done, p2_done, p3_done)):
                            sp.wait_ge(done, i + (3 if m == 2 else 1))
                            sp.dma_start(parts_d[bass.ds(i, 1), m, :, :].rearrange("a p n -> (a p) n"),
                                         part[k][:, m, :]).then_inc(stored[k], 16)
                for k in range(2):
                    sp.wait_ge(stored[k], 64 * (B // 2) + 64)


def load_stacks(sp, parts_d, i, Q, K, arrived):
    for n, (a, b) in enumerate(TERMS):
        sp.dma_start(Q[HD * n:HD * n + HD, :, :],
                     parts_d[bass.ds(i, 1), a, 0:NH * HD, :].rearrange("z (h d) t -> d (z h) t", d=HD))\
            .then_inc(arrived, 16)
        sp.dma_start(K[HD * n:HD * n + HD, :, :],
                     parts_d[bass.ds(i, 1), b, NH * HD:(NH + NKV) * HD, :].rearrange("z (h d) t -> d (z h) t", d=HD))\
            .then_inc(arrived, 16)


def max_phase(nc, P, A, parts_d, cst, max_d):
    with ExitStack() as c:
        Q = [P.sb(c, f"mq{k}", [HD * NT, NH, TP], BF16) for k in range(2)]
        K = [P.sb(c, f"mk{k}", [HD * NT, NKV, TP], BF16) for k in range(2)]
        mask = P.sb(c, "mask1", [TB, TB], BF16)
        mx = [P.sb(c, f"mx{k}", [TB, NTB, NH]) for k in range(2)]
        m4 = [P.sb(c, f"m4_{k}", [TB, 4, NH, 2]) for k in range(2)]
        m8 = [P.sb(c, f"m8_{k}", [TB, NH * 3]) for k in range(2)]
        nm = P.sb(c, "nm", [TB, B, 2, NH, NTB], BF16)
        nmT = P.sb(c, "nmT", [2 * NH * NTB, B, TB], BF16)
        mask32 = P.sb(c, "mask1f", [TB, TB])
        load_phase(nc, P, [(mask32[:], A["mask1"])], "max")
        mask_cast = P.sem("max_mask_cast")
        with nc.Block() as block:
            @block.vector
            def _(dve):
                nc.vector.tensor_copy(mask[:], mask32[:]).then_inc(mask_cast, 1)
        arrived = [P.sem(f"max_arrived{k}") for k in range(2)]
        scored, reduced, stacks_used = P.sem("max_scored"), P.sem("max_reduced"), P.sem("max_stacks_used")
        joined, hi, lo = P.sem("max_joined"), P.sem("max_hi"), P.sem("max_lo")
        units = []
        for t in range(4):
            units += [(t, [(h, 0), (h + 1, 0)], TB * (t + 1)) for h in (0, 2)]
        for t in range(4, 8):
            w = TB * (t + 1) // 2
            units += [(t, [(h, 0), (h, w)], w) for h in range(NH)]
        w8 = TB * NTB // 3
        flat = [(h, w8 * n) for h in range(NH) for n in range(3)]
        units += [(8, flat[n:n + 2], w8) for n in range(0, 12, 2)]
        NU = len(units)
        with ExitStack() as cc:
            ps = [P.ps(cc, f"max_ps{n}", [128, 2, 512]) for n in range(4)]
            with nc.Block() as block:
                @block.sync
                def _(sp):
                    with sp.Fori(0, B // 2) as j:
                        for k in range(2):
                            i = 2 * j + k
                            sp.wait_ge(stacks_used, i + 1)
                            load_stacks(sp, parts_d, i, Q[k], K[k], arrived[k])

                @block.tensor
                def _(pe):
                    pe.sem_inc(stacks_used, 2)
                    with pe.Fori(0, B // 2) as j:
                        for k in range(2):
                            i = 2 * j + k
                            pe.wait_ge(arrived[k], 32 * NT * j + 32 * NT)
                            for n, (t, pair, w) in enumerate(units):
                                slot = ps[(NU * k + n) % 4]
                                pe.wait_ge(reduced, NU * i + n + 1)
                                for b, (h, s) in enumerate(pair):
                                    q = Q[k][:, h, TB * t:TB * t + TB]
                                    edge = s + w == TB * (t + 1)
                                    last = nc.tensor.matmul(slot[0:TB, b, 0:w], q, K[k][:, h // 2, s:s + w],
                                                            start=True, stop=not edge)
                                    if edge:
                                        last = nc.tensor.matmul(slot[0:TB, b, w - TB:w], cst["ident16"][0:TB, 0:TB],
                                                                mask[:], start=False, stop=True)
                                last.then_inc(scored, 1)
                            pe.wait_ge(scored, NU * i + NU)
                            pe.sem_inc(stacks_used, 1)

                @block.vector
                def _(dve):
                    dve.sem_inc(reduced, 4)
                    with dve.Fori(0, B // 2) as j:
                        for k in range(2):
                            i = 2 * j + k
                            for n, (t, pair, w) in enumerate(units):
                                slot = ps[(NU * k + n) % 4]
                                dve.wait_ge(scored, NU * i + n + 1)
                                if t < 4:
                                    out = mx[k][:, t, pair[0][0]:pair[0][0] + 2]
                                elif t < 8:
                                    out = m4[k][:, t - 4, pair[0][0], :]
                                else:
                                    out = m8[k][:, 2 * (n - NU + 6):2 * (n - NU + 6) + 2]
                                nc.vector.tensor_reduce(out, slot[0:TB, :, 0:w], axis=AX.X, op=ALU.max)\
                                    .then_inc(reduced, 1)
                            dve.wait_ge(reduced, NU * i + NU + 4)
                            nc.vector.tensor_reduce(mx[k][:, 4:8, :], m4[k][:], axis=AX.X, op=ALU.max).then_inc(joined, 1)
                            nc.vector.tensor_reduce(mx[k][:, 8, :], m8[k][:].rearrange("p (h c) -> p h c", c=3),
                                                    axis=AX.X, op=ALU.max).then_inc(joined, 1)
                            dve.wait_ge(joined, 2 * i + 2)
                            mT = mx[k][:].rearrange("p t h -> p h t")
                            nc.vector.tensor_scalar(nm[:, i, 0, :, :], mT, -1.0, None, ALU.mult).then_inc(hi, 1)
                            dve.wait_ge(hi, i + 1)
                            nc.vector.scalar_tensor_tensor(nm[:, i, 1, :, :], mT, -1.0, nm[:, i, 0, :, :],
                                                           ALU.mult, ALU.subtract).then_inc(lo, 1)
        with ExitStack() as cc:
            NR = 2 * NH * NTB
            stat = P.sb(cc, "nm_static", [TB, 2, NR], BF16)
            pt = [P.ps(cc, f"max_pt{n}", [NR, TB], BF16) for n in range(2)]
            staged, turned, copied, stored = (P.sem(f"nm_{x}") for x in ("staged", "turned", "copied", "stored"))
            with nc.Block() as block:
                @block.scalar
                def _(act):
                    with act.Fori(0, B // 2) as j:
                        for k in range(2):
                            i = 2 * j + k
                            act.wait_ge(copied, i + 1)
                            nc.scalar.activation(stat[:, k, :], nm[:, i, :, :, :].rearrange("p a h t -> p (a h t)"),
                                                 ACT.Copy).then_inc(staged, 1)

                @block.tensor
                def _(pe):
                    with pe.Fori(0, B // 2) as j:
                        for k in range(2):
                            i = 2 * j + k
                            pe.wait_ge(staged, i + 1)
                            nc.tensor.transpose(pt[k][:], stat[:, k, :], cst["ident16"][0:TB, 0:TB]).then_inc(turned, 1)

                @block.vector
                def _(dve):
                    dve.sem_inc(copied, 2)
                    with dve.Fori(0, B // 2) as j:
                        for k in range(2):
                            i = 2 * j + k
                            dve.wait_ge(turned, i + 1)
                            nc.vector.tensor_copy(nmT[:, i, :], pt[k][:]).then_inc(copied, 1)

                @block.sync
                def _(sp):
                    sp.wait_ge(copied, B + 2)
                    sp.dma_start(max_d.rearrange("a h t b n -> (a h t) (b n)"),
                                 nmT[:].rearrange("p b n -> p (b n)")).then_inc(stored, 16)
                    sp.wait_ge(stored, 16)


def attention_phase(nc, P, A, XN, parts_d, va_d, max_d, cst):
    NR = HD * NT + 2
    with ExitStack() as c:
        Q = [P.sb(c, f"aq{k}", [NR, NH, TP], BF16) for k in range(2)]
        K = [P.sb(c, f"ak{k}", [NR, NKV, TP], BF16) for k in range(2)]
        V = [P.sb(c, f"av{k}", [128, NTB, NH * 32]) for k in range(2)]
        mask = P.sb(c, "mask2", [128, 128], BF16)
        mask32 = P.sb(c, "mask2f", [128, 128])
        wo, sel = P.sb(c, "attn_wo", [128, D]), P.sb(c, "attn_sel", [128, 128])
        prob = [P.sb(c, f"prob{n}", [128, NH, TC]) for n in range(3)]
        yv = [P.sb(c, f"yv{n}", [128, TC]) for n in range(2)]
        rec = [P.sb(c, f"rec{n}", [128, TC]) for n in range(2)]
        yn = [P.sb(c, f"yn{n}", [128, TC]) for n in range(2)]
        ps = [P.ps(c, f"att_ps{n}", [128, 2, 512]) for n in range(3)]
        av = [P.ps(c, f"att_av{n}", [128, 512]) for n in range(2)]
        load_phase(nc, P, [(mask32[:], A["mask2"]), (wo[:], A["attn_wo"]), (sel[:], A["attn_sel"])], "att")
        ones_set, mask_cast = P.sem("att_ones_set"), P.sem("att_mask_cast")
        with nc.Block() as block:
            @block.vector
            def _(dve):
                for k in range(2):
                    nc.vector.memset(K[k][HD * NT:NR, :, :], 1.0).then_inc(ones_set, 1)
                nc.vector.tensor_copy(mask[:], mask32[:]).then_inc(mask_cast, 1)
        arrived = [P.sem(f"att_arrived{k}") for k in range(2)]
        scored, expd, summed = P.sem("att_scored"), P.sem("att_exp"), P.sem("att_summed")
        y_copied, den_ready, rec_done, y_normed = (P.sem(x) for x in ("att_y_copied", "att_den_ready", "att_rec_done", "att_y_normed"))
        o_ready, o_added, used = P.sem("att_o_ready"), P.sem("att_o_added"), P.sem("att_used")
        passed = P.sem("att_passed")
        pieces = [(q, s, max(SB * s, TC * q)) for q in range(NTC) for s in range(NSB + 1) if SB * s < TC * (q + 1)]
        per = [sum(1 for p in pieces if p[0] == q) for q in range(NTC)]
        NPC = len(pieces)
        ARRIVALS = 16 * (2 * NT + 2 * NH + 1)
        NEX = 2 * NPC
        slots = []
        for q in range(NTC):
            first = sum(per[:q])
            slots += [("s", 2 * p + g) for p in range(first, first + per[q]) for g in range(2)] + [("o", q)]
        for q in range(NTC - 1):
            slots.remove(("o", q))
            slots.insert(slots.index(("s", 2 * sum(per[:q + 1]))) + 8, ("o", q))
        NS = len(slots)
        assert NS % 3 == 0

        def keys(s):
            return SB if s < NSB else 1

        with nc.Block() as block:
            @block.sync
            def _(sp):
                with sp.Fori(0, B // 2) as j:
                    for k in range(2):
                        i = 2 * j + k
                        sp.wait_ge(used, i + 1)
                        load_stacks(sp, parts_d, i, Q[k], K[k], arrived[k])
                        for a in range(2):
                            r = HD * NT + a
                            for h in range(NH):
                                sp.dma_start(Q[k][r:r + 1, h, 0:TB * NTB].rearrange("p (t n) -> p t n", n=TB),
                                             max_d[a:a + 1, h, :, i, :]).then_inc(arrived[k], 16)
                        sp.dma_start(V[k][:].rearrange("p b n -> p (b n)"),
                                     va_d[bass.ds(i, 1), :, :].rearrange("a p n -> (a p) n")).then_inc(arrived[k], 16)

            @block.tensor
            def _(pe):
                pe.sem_inc(used, 2)
                with pe.Fori(0, B // 2) as j:
                    for k in range(2):
                        i = 2 * j + k
                        pe.wait_ge(arrived[k], ARRIVALS * j + ARRIVALS)

                        def slot_free(n):
                            kind, what = slots[n - 3]
                            back = 0 if n >= 3 else 1
                            if kind == "s":
                                pe.wait_ge(expd, NEX * (i + 1 - back) + what + 1)
                            else:
                                pe.wait_ge(o_added, NTC * (i + 1 - back) + what + 1)

                        def score(n, u):
                            q, s, t0 = pieces[u // 2]
                            g, w, m = u % 2, TC * (q + 1) - t0, keys(s)
                            slot_free(n)
                            for b in range(2):
                                out = ps[n % 3]
                                a, e = t0 - SB * s, min(SB, TC * (q + 1) - SB * s)
                                edge = a < SB and s < NSB
                                last = nc.tensor.matmul(out[0:m, b, 0:w], K[k][:, g, SB * s:SB * s + m],
                                                        Q[k][:, 2 * g + b, t0:t0 + w], start=True, stop=not edge)
                                if edge:
                                    last = nc.tensor.matmul(out[0:m, b, 0:e - a], cst["ident16"], mask[:, a:e],
                                                            start=False, stop=True)
                            last.then_inc(scored, 1)

                        def weigh(p):
                            q, s, t0 = pieces[p]
                            w, m, x = TC * (q + 1) - t0, keys(s), (NTC * k + q) % 2
                            lastp = sum(per[:q + 1]) - 1
                            if s == 0:
                                pe.wait_ge(rec_done, NTC * i + q + 1)
                            wait_alone(pe, expd, NEX * (i + 1) + 2 * p + 2, passed)
                            for h in range(NH):
                                last = nc.tensor.matmul(av[x][32 * h:32 * h + 32, t0 - TC * q:TC],
                                                        V[k][0:m, s, 32 * h:32 * h + 32],
                                                        prob[p % 3][0:m, h, 0:w], start=(s == 0), stop=(p == lastp))
                            last.then_inc(summed, 1)

                        def denominators(q):
                            x = (NTC * k + q) % 2
                            pe.wait_ge(y_copied, NTC * i + q + 1)
                            nc.tensor.matmul(av[x][:, 0:TC], sel[:], yv[x][:], start=True, stop=True)\
                                .then_inc(den_ready, 1)

                        def project(n, q):
                            x = (NTC * k + q) % 2
                            slot_free(n)
                            pe.wait_ge(y_normed, NTC * i + q + 3)
                            for half in range(2):
                                a, e = max(TC * q, HP * half), min(TC * q + TC, HP * half + HP)
                                if a < e:
                                    last = nc.tensor.matmul(ps[n % 3][64 * half:64 * half + 64, 0, a - TC * q:e - TC * q],
                                                            wo[:], yn[x][:, a - TC * q:e - TC * q], start=True, stop=True)
                            last.then_inc(o_ready, 1)

                        for n, (kind, what) in enumerate(slots):
                            if kind == "s":
                                score(n, what)
                                p = what // 2
                                if what % 2 == 1 and p >= 1:
                                    weigh(p - 1)
                                for q in range(NTC - 1):
                                    if what == 2 * (sum(per[:q + 1]) + 1) + 1:
                                        denominators(q)
                            elif what < NTC - 1:
                                project(n, what)
                            else:
                                weigh(NPC - 1)
                                denominators(what)
                                project(n, what)
                        pe.wait_ge(o_ready, NTC * i + NTC)
                        pe.sem_inc(used, 1)

            @block.scalar
            def _(act):
                act.preload_act_table_set("exp_and_others")
                act.sem_inc(expd, NEX)
                with act.Fori(0, B // 2) as j:
                    for k in range(2):
                        i = 2 * j + k
                        for n, (kind, u) in enumerate(slots):
                            if kind != "s":
                                continue
                            q, s, t0 = pieces[u // 2]
                            g, w, m = u % 2, TC * (q + 1) - t0, keys(s)
                            act.wait_ge(scored, NEX * i + u + 1)
                            if g == 0:
                                act.wait_ge(summed, NPC * i + u // 2 + 1)
                            nc.scalar.activation(prob[(u // 2) % 3][0:m, 2 * g:2 * g + 2, 0:w],
                                                 ps[n % 3][0:m, :, 0:w], ACT.Exp, scale=0.25).then_inc(expd, 1)

            @block.vector
            def _(dve):
                dve.sem_inc(summed, 3)
                dve.sem_inc(rec_done, 2)
                dve.sem_inc(y_normed, 2)
                dve.sem_inc(o_added, NTC)
                with dve.Fori(0, B // 2) as j:
                    for k in range(2):
                        i = 2 * j + k
                        for q in range(NTC):
                            x = (NTC * k + q) % 2
                            dve.wait_ge(summed, NPC * i + sum(per[:q + 1]) + 3)
                            dve.wait_ge(y_normed, NTC * i + q + 1)
                            nc.vector.tensor_copy(yv[x][:], av[x][:, 0:TC]).then_inc(y_copied, 1)
                            dve.wait_ge(den_ready, NTC * i + q + 1)
                            nc.vector.reciprocal(rec[x][:], av[x][:, 0:TC]).then_inc(rec_done, 1)
                            dve.wait_ge(rec_done, NTC * i + q + 3)
                            nc.vector.tensor_tensor(yn[x][:], yv[x][:], rec[x][:], ALU.mult).then_inc(y_normed, 1)
                            dve.wait_ge(o_ready, NTC * i + q + 1)
                            slot = ps[[n for n, y in enumerate(slots) if y == ("o", q)][0] % 3]
                            flatx = XN[:, i, :, :].rearrange("p c n -> p (c n)")
                            for half in range(2):
                                a, e = max(TC * q, HP * half), min(TC * q + TC, HP * half + HP)
                                if a < e:
                                    r = slice(64 * half, 64 * half + 64)
                                    cs = slice(a - HP * half, e - HP * half)
                                    last = nc.vector.tensor_tensor(flatx[r, cs], flatx[r, cs],
                                                                   slot[r, 0, a - TC * q:e - TC * q], ALU.add)
                            last.then_inc(o_added, 1)
                dve.wait_ge(o_added, NTC * B + NTC)


def router_phase(nc, P, A, FL, cst, we_d):
    E2 = 2 * NE
    NB_ = 5
    with ExitStack() as c:
        rw, ln2 = P.sb(c, "rw", [128, E2]), P.sb(c, "ln2r", [128, 1])
        lg = [P.sb(c, f"lg{k}", [E2, NB_ * RB]) for k in range(2)]
        LT = P.sb(c, "LT", [RB, B, NB_ * E2])
        load_phase(nc, P, [(rw[:], A["rw"]), (ln2[:], A["ln2"])], "router")
        w_scaled, lg_ready, lg_copied, turned, lt_copied = (P.sem(f"rt_{x}") for x in
                                                            ("w_scaled", "lg_ready", "lg_copied", "turned", "lt_copied"))
        passed = P.sem("rt_passed")
        with ExitStack() as cc:
            lp = [P.ps(cc, f"rt_lp{k}", [E2, 2, 512]) for k in range(2)]
            tp = [P.ps(cc, f"rt_tp{k}", [RB, 512]) for k in range(2)]
            with nc.Block() as block:
                @block.vector
                def _(dve):
                    nc.vector.tensor_scalar(rw[:], rw[:], ln2[:, 0:1], None, ALU.mult).then_inc(w_scaled, 1)
                    for k in range(2):
                        nc.vector.memset(lg[k][:, HP:NB_ * RB], 0.0).then_inc(lg_copied, 1)
                    dve.sem_inc(lt_copied, 2)
                    with dve.Fori(0, B // 2) as j:
                        for k in range(2):
                            i = 2 * j + k
                            dve.wait_ge(lg_ready, i + 1)
                            dve.wait_ge(lt_copied, i + 1)
                            nc.vector.tensor_copy(lg[k][:, 0:HP].rearrange("p (c n) -> p c n", c=2),
                                                  lp[k][:, :, 0:CH]).then_inc(lg_copied, 1)

                @block.tensor
                def _(pe):
                    pe.wait_ge(w_scaled, 1)
                    with pe.Fori(0, B // 2) as j:
                        for k in range(2):
                            i = 2 * j + k
                            pe.wait_ge(lg_copied, i + 1)
                            mm2(nc, lp[k], rw[:], FL[:, i, :, :]).then_inc(lg_ready, 1)
                        for k in range(2):
                            i = 2 * j + k
                            pe.wait_ge(lg_copied, i + 3)
                            wait_alone(pe, lt_copied, i + 1, passed)
                            for b in range(NB_):
                                last = nc.tensor.transpose(tp[k][:, E2 * b:E2 * b + E2], lg[k][:, RB * b:RB * b + RB],
                                                           cst["ident"][0:E2, 0:E2])
                            last.then_inc(turned, 1)

                @block.scalar
                def _(act):
                    with act.Fori(0, B // 2) as j:
                        for k in range(2):
                            i = 2 * j + k
                            act.wait_ge(turned, i + 1)
                            nc.scalar.activation(LT[:, i, :], tp[k][:, 0:NB_ * E2], ACT.Copy).then_inc(lt_copied, 1)
        NG = B * NB_ * 2
        with ExitStack() as cc:
            m = P.sb(cc, "rt_m", [RB, NG, 1])
            den = P.sb(cc, "rt_den", [RB, NG, 1])
            top = [P.sb(cc, f"rt_top{n}", [RB, NG, 1]) for n in range(2)]
            hot = [P.sb(cc, f"rt_hot{n}", [RB, NG, NE]) for n in range(2)]
            rank = P.sb(cc, "rt_rank", [RB, NE])
            work = P.sb(cc, "rt_work", [RB, NG, NE])
            step, e_ready, e_done, rank_ready = (P.sem(f"rt_{x}") for x in ("step", "e_ready", "e_done", "rank_ready"))
            pr = LT[:].rearrange("p b (g e) -> p (b g) e", e=NE)

            def wide(x):
                return x[:].broadcast_to([RB, NG, NE])

            load_phase(nc, P, [(rank[:], A["rank"])], "rank")
            with nc.Block() as block:
                @block.scalar
                def _(act):
                    act.preload_act_table_set("exp_and_others")
                    act.wait_ge(e_ready, 1)
                    nc.scalar.activation(pr, pr, ACT.Exp).then_inc(e_done, 1)

                @block.vector
                def _(dve):
                    n = [0]

                    def then(ins):
                        n[0] += 1
                        ins.then_inc(step, 1)
                        dve.wait_ge(step, n[0])

                    v = nc.vector
                    rk = rank[:].rearrange("p (z e) -> p z e", z=1).broadcast_to([RB, NG, NE])
                    then(v.tensor_reduce(m[:], pr, axis=AX.X, op=ALU.max))
                    v.tensor_tensor(pr, pr, wide(m), ALU.subtract).then_inc(e_ready, 1)
                    dve.wait_ge(e_done, 1)
                    then(v.tensor_reduce(den[:], pr, axis=AX.X, op=ALU.add))
                    then(v.reciprocal(den[:], den[:]))
                    then(v.tensor_tensor(pr, pr, wide(den), ALU.mult))
                    for r in range(2):
                        then(v.tensor_reduce(top[r][:], pr, axis=AX.X, op=ALU.max))
                        then(v.tensor_tensor(work[:], pr, wide(top[r]), ALU.is_equal))
                        then(v.tensor_tensor(work[:], work[:], rk, ALU.mult))
                        then(v.tensor_reduce(m[:], work[:], axis=AX.X, op=ALU.max))
                        then(v.tensor_tensor(hot[r][:], work[:], wide(m), ALU.is_equal))
                        if r == 0:
                            then(v.scalar_tensor_tensor(pr, hot[0][:], -2.0, pr, ALU.mult, ALU.add))
                    then(v.tensor_tensor(den[:], top[0][:], top[1][:], ALU.add))
                    then(v.tensor_scalar(den[:], den[:], 1e-9, None, ALU.add))
                    then(v.reciprocal(den[:], den[:]))
                    for r in range(2):
                        then(v.tensor_tensor(top[r][:], top[r][:], den[:], ALU.mult))
                        then(v.tensor_tensor(hot[r][:], hot[r][:], wide(top[r]), ALU.mult))
                    then(v.tensor_tensor(pr, hot[0][:], hot[1][:], ALU.add))
        with ExitStack() as cc:
            NRW = NB_ * E2
            WT = P.sb(cc, "WT", [NRW, B, RB])
            rest = P.sb(cc, "WT_rest", [NRW, B, RB])
            parts = P.sb(cc, "WT_parts", [NRW, 3, B, RB], BF16)
            st = P.sb(cc, "rt_static", [RB, 2, NRW])
            wp = [P.ps(cc, f"rt_wp{k}", [NRW, RB]) for k in range(2)]
            staged, turned2, copied, stored = (P.sem(f"we_{x}") for x in ("staged", "turned", "copied", "stored"))
            cut_done = P.sem("we_cut")
            with nc.Block() as block:
                @block.scalar
                def _(act):
                    with act.Fori(0, B // 2) as j:
                        for k in range(2):
                            i = 2 * j + k
                            act.wait_ge(copied, i + 1)
                            nc.scalar.activation(st[:, k, :], LT[:, i, :], ACT.Copy).then_inc(staged, 1)

                @block.tensor
                def _(pe):
                    with pe.Fori(0, B // 2) as j:
                        for k in range(2):
                            i = 2 * j + k
                            pe.wait_ge(staged, i + 1)
                            nc.tensor.transpose(wp[k][:], st[:, k, :], cst["ident"][0:RB, 0:RB]).then_inc(turned2, 1)

                @block.vector
                def _(dve):
                    dve.sem_inc(copied, 2)
                    with dve.Fori(0, B // 2) as j:
                        for k in range(2):
                            i = 2 * j + k
                            dve.wait_ge(turned2, i + 1)
                            nc.vector.tensor_copy(WT[:, i, :], wp[k][:]).then_inc(copied, 1)
                    dve.wait_ge(copied, B + 2)
                    cut(nc, cut_done, dve, WT[:], parts[:, 0], rest[:], parts[:, 1], parts[:, 2], 0)

                @block.sync
                def _(sp):
                    for a, n in ((0, 1), (1, 3), (2, 4)):
                        sp.wait_ge(cut_done, n)
                        for b in range(NB_):
                            sp.dma_start(we_d[a, :, :, RB * b:RB * b + RB], parts[E2 * b:E2 * b + E2, a, :, :])\
                                .then_inc(stored, 16)
                    sp.wait_ge(stored, 16 * 3 * NB_)


def expert_phase(nc, P, A, XN, FL, h4_d, we_d, out_d):
    with ExitStack() as c:
        ws = [P.sb(c, f"ex_w{n}", [128, 3, NTL * 128], BF16) for n in range(2)]
        w2 = P.sb(c, "ex_w2", [128, NTL, D])
        spread = P.sb(c, "ex_spread", [3 * NE, NTL * 128], BF16)
        w_scaled, w_cut, spread_cast = (P.sem(f"ex_{x}") for x in ("w_scaled", "w_cut", "spread_cast"))
        with ExitStack() as cc:
            raw = [P.sb(cc, f"ex_raw{n}", [128, NTL * 128]) for n in range(2)]
            rest = P.sb(cc, "ex_rest", [128, NTL * 128])
            third = P.sb(cc, "ex_third", [128, NTL * 128], BF16)
            spread32 = P.sb(cc, "ex_spread32", [3 * NE, NTL * 128])
            ln2 = P.sb(cc, "ln2e", [128, 1])
            load_phase(nc, P, [(raw[0][:], A["ex_w1"]), (raw[1][:], A["ex_w3"]), (ln2[:], A["ln2"]),
                               (w2[:].rearrange("p t m -> p (t m)"), A["ex_w2"]), (spread32[:], A["spread"])], "ex")
            with nc.Block() as block:
                @block.vector
                def _(dve):
                    nc.vector.tensor_copy(spread[:], spread32[:]).then_inc(spread_cast, 1)
                    for n in range(2):
                        nc.vector.tensor_scalar(raw[n][:], raw[n][:], ln2[:, 0:1], None, ALU.mult).then_inc(w_scaled, 1)
                    dve.wait_ge(w_scaled, 2)
                    n = 0
                    for w, r in zip(ws, raw):
                        n = cut(nc, w_cut, dve, r[:], w[:, 0, :], rest[:], w[:, 1, :], third[:], n)
                        nc.vector.tensor_copy(w[0:64, 2, :], third[0:64, :])
                        nc.vector.tensor_copy(w[64:128, 2, :], w[64:128, 0, :]).then_inc(w_cut, 1)
                        n += 1
                        dve.wait_ge(w_cut, n)
        fl = [P.sb(c, f"ex_fl{n}", [128, 3, HP], BF16) for n in range(2)]
        fr = P.sb(c, "ex_fr", [128, 2, CH])
        xs = [P.sb(c, f"ex_xs{n}", [128, 2, TP], BF16) for n in range(2)]
        we = [P.sb(c, f"ex_we{n}", [3 * NE, TP], BF16) for n in range(2)]
        sl = [P.sb(c, f"ex_sl{n}", [128, 2, CH]) for n in range(2)]
        hu = [P.sb(c, f"ex_hu{n}", [128, 2, CH]) for n in range(4)]
        h4 = [P.sb(c, f"ex_h4{n}", [128, HP]) for n in range(2)]
        gp, up, wp, y = (P.ps(c, f"ex_{x}p", [128, 2, 512]) for x in ("g", "u", "w", "y"))
        part_done, xs_ready = P.sem("ex_part_done"), [P.sem(f"ex_xs_ready{n}") for n in range(2)]
        h4_ready = [P.sem(f"ex_h4_ready{n}") for n in range(2)]
        g_ready, u_ready, w_ready = (P.sem(f"ex_{x}_ready") for x in ("g", "u", "w"))
        silu_done, gated, weighted = (P.sem(f"ex_{x}") for x in ("silu_done", "gated", "weighted"))
        down, y_read, r_ready, image_read = (P.sem(f"ex_{x}") for x in ("down", "y_read", "r_ready", "image_read"))
        stored = [P.sem(f"ex_stored{n}") for n in range(2)]
        passed = P.sem("ex_passed")
        outv = out_d.rearrange("p (b n) -> p b n", b=B)
        h4v = h4_d.rearrange("p (b n) -> p b n", b=B)
        NLD = 16 * (8 + 6)
        NU = 2 * NTL
        with nc.Block() as block:
            @block.gpsimd
            def _(pool):
                for k in range(2):
                    pool.sem_inc(xs_ready[k], NLD)
                with pool.Fori(0, B // 2) as j:
                    for k in range(2):
                        i = 2 * j + k
                        f = [fl[k][:, m, :].rearrange("p (c n) -> p c n", c=2) for m in range(3)]
                        wait_alone(pool, xs_ready[k], NLD * j + NLD, passed)
                        nc.gpsimd.tensor_copy(f[0], FL[:, i, :, :]).then_inc(part_done, 1)
                        wait_alone(pool, part_done, 4 * i + 1, passed)
                        nc.gpsimd.tensor_tensor(fr[:], FL[:, i, :, :], f[0], op=ALU.subtract).then_inc(part_done, 1)
                        wait_alone(pool, part_done, 4 * i + 2, passed)
                        nc.gpsimd.tensor_copy(f[1], fr[:]).then_inc(part_done, 1)
                        wait_alone(pool, part_done, 4 * i + 3, passed)
                        nc.gpsimd.tensor_tensor(f[2], fr[:], f[1], op=ALU.subtract).then_inc(part_done, 1)
                        wait_alone(pool, part_done, 4 * i + 4, passed)
                        wait_alone(pool, h4_ready[k], 16 * j + 16, passed)
                        h4c = h4[k][:].rearrange("p (c n) -> p c n", c=2)
                        nc.gpsimd.tensor_tensor(h4c, XN[:, i, :, :], h4c, op=ALU.add).then_inc(r_ready, 1)

            @block.sync
            def _(sp):
                with sp.Fori(0, B // 2) as j:
                    for k in range(2):
                        i = 2 * j + k
                        sp.wait_ge(image_read, i + 1)
                        for a in range(3):
                            for h in range(2):
                                sp.dma_start(we[k][NE * a:NE * a + NE, HP * h:HP * h + HP],
                                             we_d[a, NE * h:NE * h + NE, i, 0:HP]).then_inc(xs_ready[k], 16)
                        sp.wait_ge(stored[k], 16 * j + 16)
                        sp.dma_start(h4[k][:], h4v[:, i, :]).then_inc(h4_ready[k], 16)
                        sp.wait_ge(part_done, 4 * i + 4)
                        for s, r, a in ((0, 0, 0), (0, 64, 1), (1, 0, 0), (1, 64, 2)):
                            for h in range(2):
                                sp.dma_start(xs[k][r:r + 64, s, HP * h:HP * h + HP],
                                             fl[k][64 * h:64 * h + 64, a, :]).then_inc(xs_ready[k], 16)

            @block.tensor
            def _(pe):
                pe.sem_inc(image_read, 2)
                with pe.Fori(0, B // 2) as j:
                    for k in range(2):
                        i = 2 * j + k
                        pe.wait_ge(xs_ready[k], NLD * j + 2 * NLD)

                        def three(out, w, t, h):
                            for q in range(2):
                                s = HP * h + CH * q
                                for m in range(3):
                                    last = nc.tensor.matmul(out[:, q, 0:CH], w[:, m, 128 * t:128 * t + 128],
                                                            xs[k][:, m // 2, s:s + CH], start=m == 0, stop=m == 2)
                            return last

                        def second(t, q):
                            if q == 0:
                                pe.wait_ge(weighted, NU * i + 2 * t + 2 + 4)
                                if t == 0:
                                    pe.wait_ge(y_read, i + 1)
                            for h in range(2):
                                last = nc.tensor.matmul(y[64 * h:64 * h + 64, q, 0:CH], w2[:, t, :],
                                                        hu[2 * (t % 2) + h][:, q, :], start=t == 0, stop=t == NTL - 1)
                            if q == 1:
                                last.then_inc(down, 1)

                        for t in range(NTL):
                            for h in range(2):
                                n = NU * i + 2 * t + h
                                pe.wait_ge(silu_done, n + 1)
                                three(gp, ws[0], t, h).then_inc(g_ready, 1)
                                pe.wait_ge(gated, n + 2)
                                three(up, ws[1], t, h).then_inc(u_ready, 1)
                                pe.wait_ge(weighted, n + 4)
                                for q in range(2):
                                    last = nc.tensor.matmul(wp[:, q, 0:CH], spread[:, 128 * t:128 * t + 128],
                                                            we[k][:, HP * h + CH * q:HP * h + CH * q + CH],
                                                            start=True, stop=True)
                                last.then_inc(w_ready, 1)
                                if t >= 1:
                                    second(t - 1, h)
                        pe.wait_ge(w_ready, NU * i + NU)
                        pe.sem_inc(image_read, 1)
                        for q in range(2):
                            second(NTL - 1, q)

            @block.scalar
            def _(act):
                act.preload_act_table_set("silu_and_others")
                act.sem_inc(silu_done, 1)
                for k in range(2):
                    act.sem_inc(stored[k], 16)
                with act.Fori(0, B // 2) as j:
                    for k in range(2):
                        i = 2 * j + k
                        for u in range(NU):
                            act.wait_ge(g_ready, NU * i + u + 1)
                            act.wait_ge(gated, NU * i + u + 1)
                            nc.scalar.activation(sl[u % 2][:], gp[:, :, 0:CH], ACT.Silu).then_inc(silu_done, 1)
                        act.wait_ge(y_read, i + 2)
                        act.dma_start(outv[:, i, :], h4[k][:]).then_inc(stored[k], 16)
                for k in range(2):
                    act.wait_ge(stored[k], 16 * (B // 2) + 16)

            @block.vector
            def _(dve):
                dve.sem_inc(gated, 2)
                dve.sem_inc(weighted, 4)
                dve.sem_inc(y_read, 1)
                dve.sem_inc(down, 2)
                with dve.Fori(0, B // 2) as j:
                    for k in range(2):
                        i = 2 * j + k
                        for u in range(NU):
                            n = NU * i + u
                            t, h = u // 2, u % 2
                            buf = hu[2 * (t % 2) + h]
                            dve.wait_ge(silu_done, n + 2)
                            dve.wait_ge(u_ready, n + 1)
                            if h == 0:
                                dve.wait_ge(down, NTL * i + t + 1)
                            nc.vector.tensor_tensor(buf[:], sl[u % 2][:], up[:, :, 0:CH], ALU.mult).then_inc(gated, 1)
                            dve.wait_ge(gated, n + 3)
                            dve.wait_ge(w_ready, n + 1)
                            nc.vector.tensor_tensor(buf[:], buf[:], wp[:, :, 0:CH], ALU.mult).then_inc(weighted, 1)
                        dve.wait_ge(down, NTL * i + NTL + 2)
                        dve.wait_ge(r_ready, i + 1)
                        h4c = h4[k][:].rearrange("p (c n) -> p c n", c=2)
                        nc.vector.tensor_tensor(h4c, h4c, y[:, :, 0:CH], ALU.add).then_inc(y_read, 1)


def build(nc, A, out_d):
    with ExitStack() as ctx:
        P = Place(nc)
        H = P.sb(ctx, "H", [128, B, 2, CH])
        XN = P.sb(ctx, "XN", [128, B, 2, CH])
        ident, centre, average = (P.sb(ctx, n, [128, 128]) for n in ("ident", "centre", "average"))
        ident16 = P.sb(ctx, "ident16", [128, 128], BF16)
        cst = {"ident": ident, "centre": centre[:], "average": average[:], "ident16": ident16[:]}

        def dram(name, shape, dt=F32):
            return nc.dram_tensor(name, shape, dt, kind="Internal").ap()

        wr_rows, sel_rows = dram("wr_rows", [B, 2, HP]), dram("sel_rows", [B, 2, HP])
        h4_d = dram("h4_d", [128, B * HP])
        parts_d = dram("parts_d", [B, 3, (NH + NKV) * HD, TP], BF16)
        va_d = dram("va_d", [B, 128, NTB * NH * 32])
        max_d = dram("max_d", [2, NH, NTB, B, TB], BF16)
        we_d = dram("we_d", [3, 2 * NE, B, 5 * RB], BF16)

        load_phase(nc, P, [(ident[:], A["ident"]), (centre[:], A["centre"]), (average[:], A["average"])], "common")
        ident_cast = P.sem("ident_cast")
        with nc.Block() as block:
            @block.vector
            def _(dve):
                nc.vector.tensor_copy(ident16[:], ident[:]).then_inc(ident_cast, 1)
        embed_phase(nc, P, A, H)
        P.clear()
        norm_phase(nc, P, "n1", cst, H, XN, 1e-5, True)
        P.clear()
        gate_phase(nc, P, A, H, XN)
        P.clear()
        norm_phase(nc, P, "n2", cst, H, XN, 1e-5, True)
        P.clear()
        token_weight_phase(nc, P, A, XN, wr_rows)
        P.clear()
        top_phase(nc, P, wr_rows, sel_rows)
        P.clear()
        mlp_phase(nc, P, A, H, XN, sel_rows)
        P.clear()
        norm_phase(nc, P, "n3", cst, H, XN, 1e-5, True)
        P.clear()
        rnn_phase(nc, P, A, H, XN)
        P.clear()
        norm_phase(nc, P, "n4", cst, H, XN, 1e-5, True, spill=h4_d)
        P.clear()
        norm_phase(nc, P, "n5", cst, XN, H, 1e-6, False)
        P.clear()
        qkv_phase(nc, P, A, H, cst, parts_d, va_d)
        P.clear()
        max_phase(nc, P, A, parts_d, cst, max_d)
        P.clear()
        attention_phase(nc, P, A, XN, parts_d, va_d, max_d, cst)
        P.clear()
        norm_phase(nc, P, "n6", cst, XN, H, 1e-6, False)
        P.clear()
        router_phase(nc, P, A, H, cst, we_d)
        P.clear()
        expert_phase(nc, P, A, XN, H, h4_d, we_d, out_d)
        P.clear()


def diag2(w):
    n, m = w.shape
    z = np.zeros((2 * n, 2 * m), w.dtype)
    z[:n, :m], z[n:, m:] = w, w
    return z


def layouts(x):
    f = {k: np.asarray(v) for k, v in x.items()}
    r = {}

    def col(v):
        return np.ascontiguousarray(np.tile(v.reshape(-1), 2)[:, None])

    n = 224 // 7
    p = f["x"].reshape(B, n, 7, n, 7).transpose(2, 4, 0, 1, 3).reshape(PD, B, n * n)
    z = np.zeros((PD, B, TP), np.float32)
    z[:, :, 1:T] = p
    r["patches"] = z.reshape(PD, B, 2, HP).transpose(2, 0, 1, 3).reshape(2 * PD, B * HP)
    r["wtok"] = diag2(f["L0_tok_W"].T)
    z = np.zeros((D, TP), np.float32)
    z[:, 0] = f["cls_tok"].reshape(-1)
    z[:, 1:T] = f["L0_tok_pos"][0].T
    r["pos"] = z.reshape(D, 2, HP).transpose(1, 0, 2).reshape(128, HP)
    r["tokb"] = col(f["L0_tok_b"])
    r["wg"], r["wo"] = diag2(f["L0_attn_wg"]), diag2(f["L0_attn_wo"])
    r["gnb"], r["attn_b"] = col(f["L0_attn_gn_bias"]), col(f["L0_attn_bias"])
    r["wr"] = diag2(np.repeat(f["L0_ffn_wr"], D, axis=1))
    r["br"] = np.repeat(f["L0_ffn_br"], 128)[:, None]
    w1, w2 = f["L0_ffn_w1"], f["L0_ffn_w2"]
    r["w1"] = np.stack([diag2(w1[:, D * m:D * m + D]) for m in range(4)], 1)
    r["w2"] = np.stack([diag2(w2[D * m:D * m + D]) for m in range(4)], 1)
    r["b1"] = np.tile(f["L0_ffn_b1"].reshape(4, D).T, (2, 1))
    r["b2"] = col(f["L0_ffn_b2"])
    r["wih"], r["whh"] = diag2(f["L1_attn_W_ih"].T), diag2(f["L1_attn_W_hh"].T)
    r["bih"], r["bhh"] = col(f["L1_attn_b_ih"]), col(f["L1_attn_b_hh"])
    wqkv = np.concatenate([f["L1_ffn_wq"].T, f["L1_ffn_wk"].T, f["L1_ffn_wv"].T], 1)
    turn = np.concatenate([np.roll(np.arange(HD), -HD // 2) + HD * h for h in range(8)])
    both = np.stack([wqkv, wqkv[:, turn]], 1)
    z = np.zeros((2, D, 2, 2, 128), np.float32)
    z[0, :, 0], z[1, :, 1] = both, both
    r["wqkv"] = z.reshape(128, 512)
    r["ln1"], r["ln2"] = col(f["L1_ffn_ln1_w"]), col(f["L1_ffn_ln2_w"])
    wo = f["L1_ffn_wo"].T
    z = np.zeros((NH, 32, D), np.float32)
    z[:, 0:HD] = wo.reshape(NH, HD, D)
    r["attn_wo"] = z.reshape(128, D)
    r["rw"] = diag2(f["L1_ffn_router_w"].T)
    for name in ("w1", "w3"):
        w = np.zeros((NTL * 128, D), np.float32)
        w[0:NE * HID] = f[f"L1_ffn_{name}"].reshape(NE * HID, D)
        r[f"ex_{name}"] = np.tile(w.T, (2, 1))
    w = np.zeros((NTL * 128, D), np.float32)
    w[0:NE * HID] = f["L1_ffn_w2"].transpose(0, 2, 1).reshape(NE * HID, D)
    r["ex_w2"] = w.reshape(NTL, 128, D).transpose(1, 0, 2).reshape(128, NTL * D)
    return {k: np.ascontiguousarray(v) for k, v in r.items()}


def tables():
    r = {"ident": np.eye(128, dtype=np.float32)}
    one = np.zeros((128, 128), np.float32)
    one[:D, :D] = one[D:, D:] = 1.0 / D
    r["average"], r["centre"] = one, np.eye(128, dtype=np.float32) - one
    inv = 1.0 / 10000.0 ** (np.arange(0, HD, 2, dtype=np.float32) / HD)
    ang = np.outer(np.arange(TP, dtype=np.float32), inv)
    ang = np.concatenate([ang, ang], -1).T
    sign = np.where(np.arange(HD) < HD // 2, -1.0, 1.0).astype(np.float32)[:, None]
    r["cos"] = np.tile(np.cos(ang), (NH + NKV, 1)).astype(np.float32)
    r["sin"] = np.tile(np.sin(ang) * sign, (NH + NKV, 1)).astype(np.float32)
    a = np.arange(128)
    r["mask1"] = np.where(a[None, :TB] > a[:TB, None], NEG, 0.0).astype(np.float32)
    r["mask2"] = np.where(a[:, None] > a[None, :], NEG, 0.0).astype(np.float32)
    z = np.zeros((128, 128), np.float32)
    for h in range(NH):
        z[32 * h + HD, 32 * h:32 * h + 32] = 1.0
    r["attn_sel"] = z
    z = np.zeros((NE, NTL * 128), np.float32)
    for e in range(NE):
        z[e, HID * e:HID * e + HID] = 1.0
    r["spread"] = np.tile(z, (3, 1))
    r["rank"] = np.tile(np.arange(NE, 0, -1, dtype=np.float32), (RB, 1))
    return r


def kernel(**inputs):
    import concourse.bacc as _bacc
    from concourse.bass_utils import run_bass_kernel_spmd as _run

    nc = _bacc.Bacc("TRN2", target_bir_lowering=False, num_devices=1)
    arrays = {**layouts(inputs), **tables()}
    A = {n: nc.dram_tensor(f"in_{n}", a.shape, mybir.dt.from_np(a.dtype), kind="ExternalInput").ap()
         for n, a in arrays.items()}
    out_d = nc.dram_tensor("out_0", (128, B * HP), F32, kind="ExternalOutput").ap()
    build(nc, A, out_d)
    r = _run(nc, [{f"in_{n}": a for n, a in arrays.items()}], core_ids=[0])
    o = r.results[0]["out_0"].reshape(2, D, B, HP).transpose(2, 0, 3, 1).reshape(B, TP, D)
    return np.ascontiguousarray(o[:, :T])
```

```python
import numpy as np
import concourse.bass as bass
from concourse import mybir
from contextlib import ExitStack

F32 = mybir.dt.float32
BF16 = mybir.dt.bfloat16
ALU = mybir.AluOpType
ACT = mybir.ActivationFunctionType
AX = mybir.AxisListType

B = 32
D = 64
T = 1025
CH = 257
HP = 2 * CH
TP = 2 * HP
PD = 49
KSEL = 511
NH, NKV, HD = 4, 2, 16
TB, NTB = 114, 9
SB, NSB = 128, 8
TC, NTC = 342, 3
NE, HID = 8, 170
NTL = -(-NE * HID // 128)
RB = 103
NEG = -1.0e30
LOWEST = -3.4028234663852886e38
HUGE = 3.0e38
TERMS = [(0, 0), (0, 1), (1, 0), (1, 1), (0, 2), (2, 0)]
NT = len(TERMS)


class Place:

    def __init__(self, nc):
        self.nc = nc
        self.sems = ExitStack()
        self.used = []

    def sb(self, ctx, name, shape, dt=F32):
        return ctx.enter_context(self.nc.sbuf_tensor(name, shape, dt))

    def ps(self, ctx, name, shape, dt=F32):
        return ctx.enter_context(self.nc.psum_tensor(name, shape, dt))

    def sem(self, name):
        self.used.append(self.sems.enter_context(self.nc.semaphore(name)))
        return self.used[-1]

    def clear(self):
        used, self.used = self.used, []
        with self.nc.Block() as block:
            @block.sync
            def _(sp):
                for s in used:
                    sp.sem_clear(s)
        self.sems.close()


def wait_alone(eng, sem, value, passed):
    eng.wait_ge(sem, value)
    eng.sem_inc(passed, 1)


def mm2(nc, out, lhsT, rhs, start=True, stop=True):
    for c in range(2):
        last = nc.tensor.matmul(out[:, c, 0:CH], lhsT, rhs[:, c, :], start=start, stop=stop)
    return last


def cut(nc, step, dve, src, p1, rest, p2, p3, n):
    for ins in (lambda: nc.vector.tensor_copy(p1, src),
                lambda: nc.vector.tensor_tensor(rest, src, p1, ALU.subtract),
                lambda: nc.vector.tensor_copy(p2, rest),
                lambda: nc.vector.tensor_tensor(p3, rest, p2, ALU.subtract)):
        ins().then_inc(step, 1)
        n += 1
        dve.wait_ge(step, n)
    return n


def load_phase(nc, P, dmas, name):
    ready = P.sem(f"{name}_consts")
    with nc.Block() as block:
        @block.sync
        def _(sp):
            for dst, src in dmas:
                sp.dma_start(dst, src).then_inc(ready, 16)
            sp.wait_ge(ready, 16 * len(dmas))


def embed_phase(nc, P, A, H):
    with ExitStack() as c:
        wtok = P.sb(c, "wtok", [2 * PD, 128])
        pos = P.sb(c, "pos", [128, HP])
        tokb = P.sb(c, "tokb", [128, 1])
        patch = [P.sb(c, f"patch{k}", [2 * PD, 2, CH]) for k in range(2)]
        emb = [P.ps(c, f"emb{k}", [128, 2, 512]) for k in range(2)]
        load_phase(nc, P, [(wtok[:], A["wtok"]), (pos[:], A["pos"]), (tokb[:], A["tokb"])], "embed")
        posb_ready, patch_free = P.sem("posb_ready"), P.sem("patch_free")
        patch_ready = [P.sem(f"patch_ready{k}") for k in range(2)]
        emb_ready, emb_free = P.sem("emb_ready"), P.sem("emb_free")
        patches = A["patches"].rearrange("p (b c n) -> p b c n", b=B, c=2)
        with nc.Block() as block:
            @block.sync
            def _(sp):
                with sp.Fori(0, B // 2) as j:
                    for k in range(2):
                        i = 2 * j + k
                        sp.wait_ge(patch_free, i + 1)
                        sp.dma_start(patch[k][:], patches[:, i, :, :]).then_inc(patch_ready[k], 16)

            @block.tensor
            def _(pe):
                pe.sem_inc(patch_free, 2)
                with pe.Fori(0, B // 2) as j:
                    for k in range(2):
                        i = 2 * j + k
                        pe.wait_ge(patch_ready[k], 16 * j + 16)
                        pe.wait_ge(emb_free, i + 1)
                        last = mm2(nc, emb[k], wtok[:], patch[k])
                        last.then_inc(emb_ready, 1)
                        pe.wait_ge(emb_ready, i + 1)
                        pe.sem_inc(patch_free, 1)

            @block.vector
            def _(dve):
                nc.vector.tensor_scalar(pos[0:64, 1:HP], pos[0:64, 1:HP], tokb[0:64, 0:1], None, ALU.add)
                nc.vector.tensor_scalar(pos[64:128, :], pos[64:128, :], tokb[64:128, 0:1], None,
                                        ALU.add).then_inc(posb_ready, 1)
                dve.wait_ge(posb_ready, 1)
                dve.sem_inc(emb_free, 2)
                pos2 = pos[:].rearrange("p (c n) -> p c n", c=2)
                with dve.Fori(0, B // 2) as j:
                    for k in range(2):
                        i = 2 * j + k
                        dve.wait_ge(emb_ready, i + 1)
                        nc.vector.tensor_tensor(H[:, i, :, :], emb[k][:, :, 0:CH], pos2,
                                                ALU.add).then_inc(emb_free, 1)


def norm_phase(nc, P, name, cst, src, dst, eps, centre, spill=None):
    with ExitStack() as c:
        sq = [P.sb(c, f"{name}_sq{k}", [128, 2, CH]) for k in range(2)]
        lg = [P.sb(c, f"{name}_lg{k}", [128, 2, CH]) for k in range(2)]
        rs = [P.sb(c, f"{name}_rs{k}", [128, 2, CH]) for k in range(2)]
        cen = [P.ps(c, f"{name}_cen{k}", [128, 2, 512]) for k in range(2)]
        var = [P.ps(c, f"{name}_var{k}", [128, 2, 512]) for k in range(2)]
        centred, squared, var_ready = (P.sem(f"{name}_{x}") for x in ("centred", "squared", "var_ready"))
        var_read, rstd_ready, normed = (P.sem(f"{name}_{x}") for x in ("var_read", "rstd_ready", "normed"))
        spilled, copied = P.sem(f"{name}_spilled"), P.sem(f"{name}_copied")
        with nc.Block() as block:
            if spill is not None:
                @block.sync
                def _(sp):
                    sp.dma_start(spill, src[:].rearrange("p b c n -> p (b c n)")).then_inc(spilled, 16)
                    sp.wait_ge(spilled, 16)

            def staged(eng, first, second, lead):
                for i in range(lead):
                    first(i, i % 2)
                with eng.Fori(0, B // 2 - 1) as j:
                    for k in range(2):
                        first(2 * j + k + lead, (k + lead) % 2)
                        second(2 * j + k, k)
                for i in (B - 2, B - 1):
                    if i + lead < B:
                        first(i + lead, (i + lead) % 2)
                    second(i, i % 2)

            @block.tensor
            def _(pe):
                def centre_it(i, k):
                    if centre:
                        pe.wait_ge(copied, i + 1)
                        mm2(nc, cen[k], cst["centre"], src[:, i, :, :]).then_inc(centred, 1)

                def variance(i, k):
                    pe.wait_ge(squared, i + 3)
                    pe.wait_ge(var_read, i + 1)
                    mm2(nc, var[k], cst["average"], sq[k]).then_inc(var_ready, 1)

                pe.sem_inc(var_ready, 2)
                staged(pe, centre_it, variance, 2)

            @block.scalar
            def _(act):
                def square(i, k):
                    if centre:
                        act.wait_ge(copied, i + 3)
                        nc.scalar.activation(sq[k][:], dst[:, i, :, :], ACT.Square).then_inc(squared, 1)

                def root(i, k):
                    act.wait_ge(var_ready, i + 3)
                    nc.scalar.activation(lg[k][:], var[k][:, :, 0:CH], ACT.Ln, bias=eps).then_inc(var_read, 1)
                    act.wait_ge(var_read, i + 3)
                    act.wait_ge(normed, i + 1)
                    nc.scalar.activation(rs[k][:], lg[k][:], ACT.Exp, scale=-0.5).then_inc(rstd_ready, 1)

                act.preload_act_table_set("natural_log_exp_and_others")
                act.sem_inc(var_read, 2)
                staged(act, square, root, 1)

            @block.vector
            def _(dve):
                def take(i, k):
                    if centre:
                        dve.wait_ge(centred, i + 1)
                        nc.vector.tensor_copy(dst[:, i, :, :], cen[k][:, :, 0:CH]).then_inc(copied, 1)
                    else:
                        dve.wait_ge(var_ready, i + 1)
                        nc.vector.tensor_tensor(sq[k][:], src[:, i, :, :], src[:, i, :, :], ALU.mult)\
                            .then_inc(squared, 1)

                def scale(i, k):
                    dve.wait_ge(rstd_ready, i + 1)
                    left = (dst if centre else src)[:, i, :, :]
                    nc.vector.tensor_tensor(dst[:, i, :, :], left, rs[k][:], ALU.mult).then_inc(normed, 1)

                dve.sem_inc(normed, 2)
                dve.sem_inc(squared, 2)
                dve.sem_inc(copied, 2)
                staged(dve, take, scale, 2)


def gate_phase(nc, P, A, H, XN):
    with ExitStack() as c:
        wg, wo = P.sb(c, "gate_wg", [128, 128]), P.sb(c, "gate_wo", [128, 128])
        gnb, ab = P.sb(c, "gate_gnb", [128, 1]), P.sb(c, "gate_ab", [128, 1])
        sl = [P.sb(c, f"gate_sl{k}", [128, 2, CH]) for k in range(2)]
        g = [P.ps(c, f"gate_g{k}", [128, 2, 512]) for k in range(2)]
        y = [P.ps(c, f"gate_y{k}", [128, 2, 512]) for k in range(2)]
        load_phase(nc, P, [(wg[:], A["wg"]), (wo[:], A["wo"]), (gnb[:], A["gnb"]), (ab[:], A["attn_b"])], "gate")
        wo_scaled, g_ready, silu_ready = (P.sem(f"gate_{x}") for x in ("wo_scaled", "g_ready", "silu_ready"))
        y_ready, y_added = P.sem("gate_y_ready"), P.sem("gate_y_added")
        with nc.Block() as block:
            @block.tensor
            def _(pe):
                pe.wait_ge(wo_scaled, 1)
                with pe.Fori(0, B // 2) as j:
                    for k in range(2):
                        i = 2 * j + k
                        pe.wait_ge(y_added, i + 1)
                        mm2(nc, g[k], wg[:], XN[:, i, :, :]).then_inc(g_ready, 1)
                    for k in range(2):
                        i = 2 * j + k
                        pe.wait_ge(silu_ready, i + 1)
                        mm2(nc, y[k], wo[:], sl[k]).then_inc(y_ready, 1)

            @block.scalar
            def _(act):
                act.preload_act_table_set("silu_and_others")
                with act.Fori(0, B // 2) as j:
                    for k in range(2):
                        i = 2 * j + k
                        act.wait_ge(g_ready, i + 1)
                        nc.scalar.activation(sl[k][:], g[k][:, :, 0:CH], ACT.Silu).then_inc(silu_ready, 1)

            @block.vector
            def _(dve):
                nc.vector.tensor_scalar(wo[:], wo[:], gnb[:, 0:1], None, ALU.mult).then_inc(wo_scaled, 1)
                dve.sem_inc(y_added, 2)
                with dve.Fori(0, B // 2) as j:
                    for k in range(2):
                        i = 2 * j + k
                        dve.wait_ge(y_ready, i + 1)
                        nc.vector.scalar_tensor_tensor(H[:, i, :, :], y[k][:, :, 0:CH], ab[:, 0:1], H[:, i, :, :],
                                                       ALU.add, ALU.add).then_inc(y_added, 1)


def token_weight_phase(nc, P, A, XN, wr_rows):
    with ExitStack() as c:
        wr, br = P.sb(c, "wr", [128, 128]), P.sb(c, "br", [128, 1])
        row = [P.sb(c, f"wr_row{k}", [128, 2, CH]) for k in range(2)]
        w = [P.ps(c, f"wr_ps{k}", [128, 2, 512]) for k in range(2)]
        load_phase(nc, P, [(wr[:], A["wr"]), (br[:], A["br"])], "wr")
        w_ready, w_copied = P.sem("wr_ready"), P.sem("wr_copied")
        stored = [P.sem(f"wr_stored{k}") for k in range(2)]
        with nc.Block() as block:
            @block.tensor
            def _(pe):
                with pe.Fori(0, B // 2) as j:
                    for k in range(2):
                        i = 2 * j + k
                        pe.wait_ge(w_copied, i + 1)
                        mm2(nc, w[k], wr[:], XN[:, i, :, :]).then_inc(w_ready, 1)

            @block.scalar
            def _(act):
                act.sem_inc(w_copied, 2)
                for k in range(2):
                    act.sem_inc(stored[k], 32)
                with act.Fori(0, B // 2) as j:
                    for k in range(2):
                        i = 2 * j + k
                        act.wait_ge(w_ready, i + 1)
                        act.wait_ge(stored[k], 32 * j + 32)
                        nc.scalar.activation(row[k][:], w[k][:, :, 0:CH], ACT.Identity,
                                             bias=br[:, 0:1]).then_inc(w_copied, 1)

            @block.sync
            def _(sp):
                with sp.Fori(0, B // 2) as j:
                    for k in range(2):
                        i = 2 * j + k
                        sp.wait_ge(w_copied, i + 3)
                        for h in range(2):
                            sp.dma_start(wr_rows[bass.ds(i, 1), h, :],
                                         row[k][64 * h:64 * h + 1, :, :].rearrange("p c n -> p (c n)"))\
                                .then_inc(stored[k], 16)
                for k in range(2):
                    sp.wait_ge(stored[k], 32 * (B // 2) + 32)


def mlp_phase(nc, P, A, H, XN, wr_rows, sel_rows):
    with ExitStack() as c:
        w1, w2 = P.sb(c, "mlp_w1", [128, 4, 128]), P.sb(c, "mlp_w2", [128, 4, 128])
        b1, b2 = P.sb(c, "mlp_b1", [128, 4]), P.sb(c, "mlp_b2", [128, 1])
        act_out = [P.sb(c, f"mlp_g{k}", [128, 4, 2, CH]) for k in range(2)]
        sel = [P.sb(c, f"mlp_sel{k}", [128, 2, CH]) for k in range(2)]
        tmp = [P.sb(c, f"mlp_t{k}", [128, 2, CH]) for k in range(2)]
        w = P.sb(c, "top_w", [B, TP])
        left = P.sb(c, "top_left", [B, T + 1])
        most = P.sb(c, "top_most", [B, 8])
        u = [P.ps(c, f"mlp_u{k}", [128, 2, 512]) for k in range(2)]
        y = [P.ps(c, f"mlp_y{k}", [128, 2, 512]) for k in range(2)]
        load_phase(nc, P, [(w1[:], A["w1"]), (w2[:], A["w2"]), (b1[:], A["b1"]), (b2[:], A["b2"]),
                           (w[:], wr_rows.rearrange("b h n -> b (h n)"))], "mlp")
        u_ready, gelu_ready, y_ready, y_read = (P.sem(f"mlp_{x}") for x in ("u_ready", "gelu_ready", "y_ready", "y_read"))
        t_ready, r_ready, h_ready = P.sem("mlp_t_ready"), P.sem("mlp_r_ready"), P.sem("mlp_h_ready")
        sel_ready = [P.sem(f"mlp_sel_ready{k}") for k in range(2)]
        step, stored, passed = P.sem("top_step"), P.sem("top_stored"), P.sem("top_passed")
        ROUNDS = (KSEL + 1) // 8
        with nc.Block() as block:
            @block.sync
            def _(sp):
                sp.wait_ge(step, 2 + 2 * ROUNDS + 3)
                sp.dma_start(sel_rows.rearrange("b h n -> b (h n)"), w[:]).then_inc(stored, 16)
                sp.wait_ge(stored, 16)
                with sp.Fori(0, B // 2) as j:
                    for k in range(2):
                        i = 2 * j + k
                        sp.wait_ge(t_ready, i + 1)
                        for h in range(2):
                            sp.dma_start(sel[k][64 * h:64 * h + 64, :, :].rearrange("p c n -> p (c n)"),
                                         sel_rows[bass.ds(i, 1), h, :].broadcast_to([64, HP]))\
                                .then_inc(sel_ready[k], 16)

            @block.tensor
            def _(pe):
                with pe.Fori(0, B // 2) as j:
                    for k in range(2):
                        i = 2 * j + k
                        for m in range(4):
                            pe.wait_ge(gelu_ready, 4 * i + m + 1)
                            mm2(nc, u[m % 2], w1[:, m, :], XN[:, i, :, :]).then_inc(u_ready, 1)
                    for k in range(2):
                        i = 2 * j + k
                        pe.wait_ge(gelu_ready, 4 * i + 6)
                        pe.wait_ge(y_read, i + 1)
                        for m in range(4):
                            last = mm2(nc, y[k], w2[:, m, :], act_out[k][:, m, :, :], m == 0, m == 3)
                        last.then_inc(y_ready, 1)

            @block.scalar
            def _(act):
                act.preload_act_table_set("gelu_apprx_tanh_and_others")
                act.sem_inc(gelu_ready, 2)
                act.sem_inc(y_read, 2)
                with act.Fori(0, B // 2) as j:
                    for k in range(2):
                        i = 2 * j + k
                        for m in range(4):
                            act.wait_ge(u_ready, 4 * i + m + 1)
                            nc.scalar.activation(act_out[k][:, m, :, :], u[m % 2][:, :, 0:CH], ACT.Gelu_apprx_tanh,
                                                 bias=b1[:, m:m + 1]).then_inc(gelu_ready, 1)
                    for k in range(2):
                        i = 2 * j + k
                        act.wait_ge(y_ready, i + 1)
                        act.wait_ge(r_ready, i + 1)
                        nc.scalar.activation(XN[:, i, :, :], y[k][:, :, 0:CH], ACT.Identity,
                                             bias=b2[:, 0:1]).then_inc(y_read, 1)

            @block.gpsimd
            def _(pool):
                with pool.Fori(0, B // 2) as j:
                    for k in range(2):
                        i = 2 * j + k
                        nc.gpsimd.tensor_tensor(H[:, i, :, :], H[:, i, :, :], XN[:, i, :, :], op=ALU.add)\
                            .then_inc(r_ready, 1)

            @block.vector
            def _(dve):
                nc.vector.memset(left[:, T:T + 1], HUGE).then_inc(step, 1)
                nc.vector.tensor_copy(left[:, 0:T], w[:, 0:T]).then_inc(step, 1)
                with dve.Fori(0, ROUNDS) as r:
                    wait_alone(dve, step, 2 * r + 2, passed)
                    nc.vector.max(most[:], left[:]).then_inc(step, 1)
                    wait_alone(dve, step, 2 * r + 3, passed)
                    nc.vector.match_replace(left[:], most[:], left[:], LOWEST).then_inc(step, 1)
                dve.wait_ge(step, 2 + 2 * ROUNDS)
                nc.vector.tensor_tensor(left[:, 0:T], left[:, 0:T], w[:, 0:T], ALU.not_equal).then_inc(step, 1)
                dve.wait_ge(step, 2 + 2 * ROUNDS + 1)
                nc.vector.tensor_tensor(w[:, 0:T], left[:, 0:T], w[:, 0:T], ALU.mult).then_inc(step, 1)
                nc.vector.memset(w[:, T:TP], 0.0).then_inc(step, 1)
                dve.sem_inc(t_ready, 2)
                dve.sem_inc(h_ready, 2)
                with dve.Fori(0, B // 2) as j:
                    for k in range(2):
                        i = 2 * j + k
                        dve.wait_ge(y_read, i + 3)
                        dve.wait_ge(sel_ready[k], 32 * j + 32)
                        dve.wait_ge(h_ready, i + 1)
                        nc.vector.tensor_tensor(tmp[k][:], XN[:, i, :, :], sel[k][:], ALU.mult).then_inc(t_ready, 1)
                    for k in range(2):
                        i = 2 * j + k
                        dve.wait_ge(t_ready, i + 3)
                        dve.wait_ge(r_ready, i + 1)
                        nc.vector.tensor_tensor(H[:, i, :, :], H[:, i, :, :], tmp[k][:], ALU.add).then_inc(h_ready, 1)
                dve.wait_ge(h_ready, B + 2)


def rnn_phase(nc, P, A, H, XN):
    with ExitStack() as c:
        wih, whh = P.sb(c, "wih", [128, 128]), P.sb(c, "whh", [128, 128])
        bih, bhh = P.sb(c, "bih", [128, 1]), P.sb(c, "bhh", [128, 1])
        hid = [P.sb(c, f"hid{k}", [128, 2, CH]) for k in range(2)]
        z = [P.ps(c, f"rnn_z{k}", [128, 2, 512]) for k in range(2)]
        load_phase(nc, P, [(wih[:], A["wih"]), (whh[:], A["whh"]), (bih[:], A["bih"]), (bhh[:], A["bhh"])], "rnn")
        bias_ready, z_ready = P.sem("rnn_bias_ready"), [P.sem(f"rnn_z_ready{q}") for q in range(2)]
        tanh_done, added = [P.sem(f"rnn_tanh{q}") for q in range(2)], P.sem("rnn_added")
        with nc.Block() as block:
            @block.tensor
            def _(pe):
                with pe.Fori(0, B // 2) as j:
                    for k in range(2):
                        i = 2 * j + k
                        for q in range(2):
                            nc.tensor.matmul(z[k][:, q, 0:CH], wih[:], XN[:, i, q, :], start=True, stop=False)
                        for q in range(2):
                            pe.wait_ge(tanh_done[q], i + 1)
                            nc.tensor.matmul(z[k][:, q, 0:CH], whh[:], hid[1 - k][:, q, :], start=False, stop=True)\
                                .then_inc(z_ready[q], 1)

            @block.scalar
            def _(act):
                act.preload_act_table_set("exp_and_others")
                act.wait_ge(bias_ready, 1)
                with act.Fori(0, B // 2) as j:
                    for k in range(2):
                        i = 2 * j + k
                        for q in range(2):
                            act.wait_ge(z_ready[q], i + 1)
                            act.wait_ge(added, i + 1)
                            nc.scalar.activation(hid[k][:, q, :], z[k][:, q, 0:CH], ACT.Tanh, bias=bih[:, 0:1])\
                                .then_inc(tanh_done[q], 1)

            @block.vector
            def _(dve):
                nc.vector.tensor_tensor(bih[:], bih[:], bhh[:], ALU.add).then_inc(bias_ready, 1)
                for q in range(2):
                    nc.vector.memset(hid[1][:, q, :], 0.0).then_inc(tanh_done[q], 1)
                dve.sem_inc(added, 2)
                with dve.Fori(0, B // 2) as j:
                    for k in range(2):
                        i = 2 * j + k
                        for q in range(2):
                            dve.wait_ge(tanh_done[q], i + 2)
                        nc.vector.tensor_tensor(H[:, i, :, :], H[:, i, :, :], hid[k][:], ALU.add).then_inc(added, 1)


def qkv_phase(nc, P, A, HN, cst, parts_d, va_d):
    NQK = (NH + NKV) * HD
    with ExitStack() as c:
        wq = P.sb(c, "wqkv", [128, 2, 2, 128])
        ln1 = P.sb(c, "ln1", [128, 1])
        cos, sin = P.sb(c, "cos", [NQK, TP]), P.sb(c, "sin", [NQK, TP])
        qc = [P.sb(c, f"qc{k}", [NQK, TP]) for k in range(2)]
        qs = [P.sb(c, f"qs{k}", [NQK, TP]) for k in range(2)]
        r1 = [P.sb(c, f"r1_{k}", [NQK, TP]) for k in range(2)]
        part = [P.sb(c, f"part{k}", [NQK, 3, TP], BF16) for k in range(2)]
        vt = [P.sb(c, f"vt{k}", [128, TP]) for k in range(2)]
        va = [P.sb(c, f"va{k}", [128, NTB, NH, 32]) for k in range(2)]
        plain = [P.ps(c, f"plain{h}", [128, 2, 512]) for h in range(2)]
        turned = [P.ps(c, f"turned{h}", [128, 512]) for h in range(2)]
        vtp = [P.ps(c, f"vtp{h}", [128, 512]) for h in range(2)]
        load_phase(nc, P, [(wq[:].rearrange("p a b m -> p (a b m)"), A["wqkv"]), (ln1[:], A["ln1"]),
                           (cos[:], A["cos"]), (sin[:], A["sin"])], "qkv")
        w_scaled, ones_set = P.sem("qkv_w_scaled"), P.sem("va_ones")
        plain_ready, turned_ready = P.sem("plain_ready"), P.sem("turned_ready")
        cos_done, sin_done, v_copied = P.sem("cos_done"), P.sem("sin_done"), P.sem("v_copied")
        sum_done, p1_done, d1_done, p2_done, p3_done = (P.sem(x) for x in ("qk_sum", "part1", "rest1", "part2", "part3"))
        v_turned, va_done = P.sem("v_turned"), P.sem("va_done")
        stored = [P.sem(f"qkv_stored{k}") for k in range(2)]
        passed = P.sem("qkv_passed")
        with nc.Block() as block:
            @block.vector
            def _(dve):
                nc.vector.tensor_scalar(wq[:], wq[:], ln1[:, 0:1], None, ALU.mult).then_inc(w_scaled, 1)
                for k in range(2):
                    nc.vector.memset(va[k][:, :, :, HD:32], 1.0).then_inc(ones_set, 1)
                    nc.vector.memset(va[k][:, NTB - 1, :, 0:HD], 0.0).then_inc(ones_set, 1)
                dve.wait_ge(ones_set, 4)
                dve.sem_inc(cos_done, 2)
                dve.sem_inc(sin_done, 2)
                dve.sem_inc(va_done, 2)

                def turn_parts(i, j, k):
                    for h in range(2):
                        for q in range(2):
                            s = slice(HP * h + CH * q, HP * h + CH * q + CH)
                            if q == 0:
                                dve.wait_ge(plain_ready, 2 * i + h + 1)
                                if h == 0:
                                    dve.wait_ge(p3_done, i + 1)
                                nc.vector.tensor_tensor(
                                    qc[k][:, HP * h:HP * h + HP].rearrange("p (c n) -> p c n", c=2),
                                    plain[h][0:NQK, :, 0:CH],
                                    cos[:, HP * h:HP * h + HP].rearrange("p (c n) -> p c n", c=2),
                                    ALU.mult).then_inc(cos_done, 1)
                            dve.wait_ge(turned_ready, 4 * i + 2 * h + q + 1)
                            nc.vector.tensor_tensor(qs[k][:, s], turned[q][0:NQK, 0:CH], sin[:, s],
                                                    ALU.mult).then_inc(sin_done, 1)
                    dve.wait_ge(cos_done, 2 * i + 4)
                    dve.wait_ge(sin_done, 4 * i + 6)
                    nc.vector.tensor_tensor(qc[k][:], qc[k][:], qs[k][:], ALU.add).then_inc(sum_done, 1)

                def copy_v(i, j, k):
                    dve.wait_ge(v_turned, i + 1)
                    dve.wait_ge(stored[k], 64 * j + 64)
                    vv = vtp[k][:, 0:NSB * 32].rearrange("p (b g d) -> p b g d", b=NSB, g=NKV)
                    for r in range(2):
                        nc.vector.tensor_copy(va[k][:, 0:NSB, r:NH:2, 0:HD], vv)
                        last = nc.vector.tensor_copy(
                            va[k][0:4, NSB, r:NH:2, 0:HD],
                            vtp[k][0:4, NSB * 32:NTB * 32].rearrange("p (g d) -> p g d", g=NKV))
                    last.then_inc(va_done, 1)

                with dve.Fori(0, B // 2) as j:
                    for k in range(2):
                        turn_parts(2 * j + k, j, k)
                        copy_v(2 * j + k, j, k)

            @block.tensor
            def _(pe):
                pe.wait_ge(w_scaled, 1)
                with pe.Fori(0, B // 2) as j:
                    for k in range(2):
                        i = 2 * j + k
                        for h in range(2):
                            pe.wait_ge(cos_done, 2 * i + h + 1)
                            pe.wait_ge(v_copied, 2 * i + h + 1)
                            mm2(nc, plain[h], wq[:, h, 0, :], HN[:, i, :, :]).then_inc(plain_ready, 1)
                            for q in range(2):
                                pe.wait_ge(sin_done, 4 * i + 2 * h + q + 1)
                                nc.tensor.matmul(turned[q][0:NQK, 0:CH], wq[:, h, 1, 0:NQK], HN[:, i, q, :],
                                                 start=True, stop=True).then_inc(turned_ready, 1)
                        pe.wait_ge(v_copied, 2 * i + 4)
                        wait_alone(pe, va_done, i + 1, passed)
                        for b in range(NTB):
                            n = min(128, TP - 128 * b)
                            last = nc.tensor.transpose(vtp[k][0:n, 32 * b:32 * b + 32],
                                                       vt[k][96:128, 128 * b:128 * b + n],
                                                       cst["ident"][96:128, 96:128])
                        last.then_inc(v_turned, 1)

            @block.scalar
            def _(act):
                act.sem_inc(v_copied, 2)

                def copy_v(i, k):
                    for h in range(2):
                        act.wait_ge(plain_ready, 2 * i + h + 1)
                        act.wait_ge(va_done, i + 1)
                        nc.scalar.activation(
                            vt[k][96:128, HP * h:HP * h + HP].rearrange("p (c n) -> p c n", c=2),
                            plain[h][96:128, :, 0:CH], ACT.Copy).then_inc(v_copied, 1)

                def first_part(i, j, k):
                    act.wait_ge(sum_done, i + 1)
                    act.wait_ge(stored[k], 64 * j + 64)
                    nc.scalar.activation(part[k][:, 0, :], qc[k][:], ACT.Copy).then_inc(p1_done, 1)

                def second_part(i, k):
                    act.wait_ge(d1_done, i + 3)
                    nc.scalar.activation(part[k][:, 1, :], r1[k][:], ACT.Copy).then_inc(p2_done, 1)

                def image(i, j, k):
                    copy_v(i, k)
                    second_part(i - 1, 1 - k)
                    first_part(i, j, k)

                copy_v(0, 0)
                first_part(0, 0, 0)
                with act.Fori(0, B // 2 - 1) as j:
                    image(2 * j + 1, j, 1)
                    image(2 * j + 2, j + 1, 0)
                image(B - 1, B // 2 - 1, 1)
                second_part(B - 1, 1)

            @block.gpsimd
            def _(pool):
                pool.sem_inc(d1_done, 2)
                pool.sem_inc(p3_done, 2)
                with pool.Fori(0, B // 2) as j:
                    for k in range(2):
                        i = 2 * j + k
                        pool.wait_ge(p1_done, i + 1)
                        pool.wait_ge(p3_done, i + 1)
                        nc.gpsimd.tensor_tensor(r1[k][:], qc[k][:], part[k][:, 0, :], op=ALU.subtract)\
                            .then_inc(d1_done, 1)
                        pool.wait_ge(p2_done, i + 1)
                        nc.gpsimd.tensor_tensor(part[k][:, 2, :], r1[k][:], part[k][:, 1, :], op=ALU.subtract)\
                            .then_inc(p3_done, 1)

            @block.sync
            def _(sp):
                for k in range(2):
                    sp.sem_inc(stored[k], 64)
                with sp.Fori(0, B // 2) as j:
                    for k in range(2):
                        i = 2 * j + k
                        sp.wait_ge(va_done, i + 3)
                        sp.dma_start(va_d[bass.ds(i, 1), :, :].rearrange("a p n -> (a p) n"),
                                     va[k][:].rearrange("p b h d -> p (b h d)")).then_inc(stored[k], 16)
                        for m, done in enumerate((p1_done, p2_done, p3_done)):
                            sp.wait_ge(done, i + (3 if m == 2 else 1))
                            sp.dma_start(parts_d[bass.ds(i, 1), m, :, :].rearrange("a p n -> (a p) n"),
                                         part[k][:, m, :]).then_inc(stored[k], 16)
                for k in range(2):
                    sp.wait_ge(stored[k], 64 * (B // 2) + 64)


def load_stacks(sp, parts_d, i, Q, K, arrived):
    for n, (a, b) in enumerate(TERMS):
        sp.dma_start(Q[HD * n:HD * n + HD, :, :],
                     parts_d[bass.ds(i, 1), a, 0:NH * HD, :].rearrange("z (h d) t -> d (z h) t", d=HD))\
            .then_inc(arrived, 16)
        sp.dma_start(K[HD * n:HD * n + HD, :, :],
                     parts_d[bass.ds(i, 1), b, NH * HD:(NH + NKV) * HD, :].rearrange("z (h d) t -> d (z h) t", d=HD))\
            .then_inc(arrived, 16)


def attention_phase(nc, P, A, XN, H, parts_d, va_d, cst):
    NR = HD * NT + 2
    NMX = 2 * NH * NTB
    with ExitStack() as c:
        Q = [P.sb(c, f"aq{k}", [NR, NH, TP], BF16) for k in range(3)]
        K = [P.sb(c, f"ak{k}", [NR, NKV, TP], BF16) for k in range(3)]
        mask1, mask2 = P.sb(c, "mask1", [TB, TB], BF16), P.sb(c, "mask2", [128, 128], BF16)
        mask1f, mask2f = P.sb(c, "mask1f", [TB, TB]), P.sb(c, "mask2f", [128, 128])
        wo, sel = P.sb(c, "attn_wo", [128, D]), P.sb(c, "attn_sel", [128, 128])
        two = P.sb(c, "two", [128, TC])
        mx = P.sb(c, "mx", [TB, NTB, NH])
        m2 = P.sb(c, "mx2", [TB, 4, NH, 2])
        m3 = P.sb(c, "mx3", [TB, NH * 3])
        nm = P.sb(c, "nm", [TB, 2, NH, NTB])
        nmh = P.sb(c, "nmh", [TB, NH, NTB], BF16)
        nmT = [P.sb(c, f"nmT{k}", [NMX, TB], BF16) for k in range(2)]
        free = H[:].rearrange("p b c n -> p (b c n)")
        at = [0]

        def carve(n):
            at[0] += n
            return free[:, at[0] - n:at[0]]

        V = [carve(NTB * NH * 32).rearrange("p (b n) -> p b n", b=NTB) for _ in range(2)]
        prob = [carve(NH * TC).rearrange("p (h n) -> p h n", h=NH) for _ in range(3)]
        yv, rec, yn, lden = ([carve(TC) for _ in range(2)] for _ in range(4))
        ps = [P.ps(c, f"att_ps{n}", [128, 2, 512]) for n in range(2)]
        mp = [P.ps(c, f"att_mp{n}", [128, 512]) for n in range(2)]
        av = [P.ps(c, f"att_av{n}", [128, 512]) for n in range(2)]
        load_phase(nc, P, [(mask1f[:], A["mask1"]), (mask2f[:], A["mask2"]), (wo[:], A["attn_wo"]),
                           (sel[:], A["attn_sel"])], "att")
        set_up = P.sem("att_set_up")
        with nc.Block() as block:
            @block.vector
            def _(dve):
                nc.vector.memset(two[:], 2.0).then_inc(set_up, 1)
                for k in range(3):
                    nc.vector.memset(K[k][HD * NT:NR, :, :], 1.0).then_inc(set_up, 1)
                nc.vector.tensor_copy(mask1[:], mask1f[:]).then_inc(set_up, 1)
                nc.vector.tensor_copy(mask2[:], mask2f[:]).then_inc(set_up, 1)
        stacks_in = [P.sem(f"att_stacks_in{k}") for k in range(3)]
        rest_in = [P.sem(f"att_rest_in{k}") for k in range(2)]
        scored, expd, summed = P.sem("att_scored"), P.sem("att_exp"), P.sem("att_summed")
        mscored, reduced, joined = P.sem("att_mscored"), P.sem("att_reduced"), P.sem("att_joined")
        hi, lo, turned, nm_copied = (P.sem(f"att_{x}") for x in ("hi", "lo", "turned", "nm_copied"))
        y_copied, den_ready, rec_done, y_normed = (P.sem(f"att_{x}") for x in ("y_copied", "den_ready", "rec_done", "y_normed"))
        ln_done, rec_ready, newton = (P.sem(f"att_{x}") for x in ("ln_done", "rec_ready", "newton"))
        o_ready, o_added, passed = P.sem("att_o_ready"), P.sem("att_o_added"), P.sem("att_passed")
        units = []
        for t in range(NTB):
            n = 1 if t < 4 else 2 if t < 8 else 3
            w = TB * (t + 1) // n
            units += [(t, h, z, w * z, w) for h in range(NH) for z in range(n)]
        NU = len(units)
        pieces = [(q, s, max(SB * s, TC * q)) for q in range(NTC) for s in range(NSB + 1) if SB * s < TC * (q + 1)]
        NPC = len(pieces)
        NEX = 2 * NPC
        ends = [max(p for p in range(NPC) if pieces[p][0] == q) for q in range(NTC)]
        S_IN, R_IN = 16 * 2 * NT, 16 * (2 * NH + 1)

        FIRST_M, LAST_M = 1, 3 * NPC - 18

        def steps(last):
            out, m = [], 0
            for p in range(NPC):
                for z, e in enumerate((("s", 2 * p), ("s", 2 * p + 1), ("w", p - 1))):
                    out.append(e)
                    while not last and m < NU and 3 * p + z >= FIRST_M + m * (LAST_M - FIRST_M) // NU:
                        out.append(("m", m))
                        m += 1
                    if not last and 3 * p + z == LAST_M:
                        out.append(("j", 0))
                    if not last and 3 * p + z == LAST_M + 3:
                        out.append(("t", 0))
                for q in range(NTC):
                    if p == ends[q - 1] + 2 if q else p == 1:
                        out.append(("d", q - 1))
                    if p == ends[q - 1] + 3 if q else p == 2:
                        out.append(("r", q - 1))
                    if p == ends[q - 1] + 5 if q else p == 4:
                        out.append(("o", q - 1))
            if last:
                out += [("w", NPC - 1), ("d", NTC - 1), ("r", NTC - 1), ("o", NTC - 1)]
            return out

        MAIN, TAIL = steps(False), steps(True)
        slots = {id(x): [e for e in x if e[0] in "sto"] for x in (MAIN, TAIL)}
        assert len(slots[id(MAIN)]) % 2 == 0 and NU % 2 == 0

        def keys(s):
            return SB if s < NSB else 1

        def every_image(run, before):
            before()
            run(0, 0, 0, 0, 0, MAIN, True)
            with run.eng.Fori(0, (B - 2) // 6) as j:
                for z in range(1, 7):
                    run(6 * j + z, z % 2, 3 * j + z // 2, z % 3, 2 * j + z // 3, MAIN, False)
            run(B - 1, (B - 1) % 2, (B - 1) // 2, (B - 1) % 3, (B - 1) // 3, TAIL, False)

        with nc.Block() as block:
            @block.sync
            def _(sp):
                def load(x, g):
                    load_stacks(sp, parts_d, x, Q[g], K[g], stacks_in[g])

                def rows(x, b, g):
                    sp.dma_start(V[b].rearrange("p b n -> p (b n)"),
                                 va_d[bass.ds(x, 1), :, :].rearrange("a p n -> (a p) n")).then_inc(rest_in[b], 16)
                    sp.wait_ge(nm_copied, x + 1)
                    for a in range(2):
                        for h in range(NH):
                            r = NTB * (NH * a + h)
                            sp.dma_start(Q[g][HD * NT + a:HD * NT + a + 1, h, 0:TB * NTB].rearrange("p (t n) -> p t n", n=TB),
                                         nmT[b][r:r + NTB, :]).then_inc(rest_in[b], 16)

                load(0, 0)
                load(1, 1)
                rows(0, 0, 0)
                load(2, 2)
                rows(1, 1, 1)
                def next_image(x, z, more):
                    sp.wait_ge(summed, NPC * (x - 1) + 3)
                    if more:
                        load(x + 1, z % 3)
                    rows(x, z % 2, (z + 2) % 3)

                with sp.Fori(0, (B - 2) // 6 - 1) as j:
                    for z in range(6):
                        next_image(6 * j + z + 2, z, True)
                for z in range(6):
                    next_image(B - 6 + z, z, z < 5)

            @block.tensor
            def _(pe):
                def top_unit(n, x, g, wait):
                    t, h, z, s, w = units[n]
                    slot = mp[n % 2]
                    if wait:
                        pe.wait_ge(reduced, NU * x + n - 1)
                    edge = s + w == TB * (t + 1)
                    last = nc.tensor.matmul(slot[0:TB, 0:w], Q[g][0:HD * NT, h, TB * t:TB * t + TB],
                                            K[g][0:HD * NT, h // 2, s:s + w], start=True, stop=not edge)
                    if edge:
                        last = nc.tensor.matmul(slot[0:TB, w - TB:w], cst["ident16"][0:TB, 0:TB],
                                                mask1[:], start=False, stop=True)
                    last.then_inc(mscored, 1)

                def turn(slot, x):
                    pe.wait_ge(lo, x + 1)
                    nc.tensor.transpose(slot[0:NMX, 0, 0:TB], nm[:].rearrange("p a h t -> p (a h t)"),
                                        cst["ident"][0:TB, 0:TB]).then_inc(turned, 1)

                def before():
                    pe.wait_ge(stacks_in[0], S_IN)
                    for n in range(NU):
                        top_unit(n, 0, 0, n >= 2)
                    turn(ps[1], 0)

                def image(i, b, half, g, third, order, first):
                    mine = slots[id(order)]

                    def slot_free(n):
                        kind, what = mine[n - 2] if n >= 2 else slots[id(MAIN)][n - 2]
                        img = i if n >= 2 else i - 1
                        if kind == "s":
                            pe.wait_ge(expd, NEX * (img + 1) + what + 1)
                        elif kind == "o":
                            pe.wait_ge(o_added, NTC * (img + 1) + what + 1)
                        else:
                            pe.wait_ge(nm_copied, img + 2)

                    def score(slot, u):
                        q, s, t0 = pieces[u // 2]
                        kv, w, m = u % 2, TC * (q + 1) - t0, keys(s)
                        for z in range(2):
                            a, e = t0 - SB * s, min(SB, TC * (q + 1) - SB * s)
                            edge = a < SB and s < NSB
                            last = nc.tensor.matmul(slot[0:m, z, 0:w], K[g][:, kv, SB * s:SB * s + m],
                                                    Q[g][:, 2 * kv + z, t0:t0 + w], start=True, stop=not edge)
                            if edge:
                                last = nc.tensor.matmul(slot[0:m, z, 0:e - a], cst["ident16"], mask2[:, a:e],
                                                        start=False, stop=True)
                        last.then_inc(scored, 1)

                    def weigh(p):
                        v = V[b] if p >= 0 else V[1 - b]
                        q, s, t0 = pieces[p]
                        x = (NTC * b + (q if p >= 0 else -1)) % 2
                        w, m = TC * (q + 1) - t0, keys(s)
                        if s == 0:
                            pe.wait_ge(rec_done, NTC * i + q + 1)
                        wait_alone(pe, expd, NEX * (i + 1) + 2 * p + 2, passed)
                        for h in range(NH):
                            last = nc.tensor.matmul(av[x][32 * h:32 * h + 32, t0 - TC * q:TC],
                                                    v[0:m, s, 32 * h:32 * h + 32],
                                                    prob[p % 3][0:m, h, 0:w], start=(s == 0), stop=(p % NPC in ends))
                        last.then_inc(summed, 1)

                    def denominators(q):
                        x = (NTC * b + q) % 2
                        pe.wait_ge(y_copied, NTC * i + q + 1)
                        nc.tensor.matmul(av[x][:, 0:TC], sel[:], yv[x], start=True, stop=True).then_inc(den_ready, 1)

                    def project(slot, q):
                        x, t0 = (NTC * b + q) % 2, TC * (q % NTC)
                        pe.wait_ge(y_normed, NTC * i + q + 3)
                        for hf in range(2):
                            a, e = max(t0, HP * hf), min(t0 + TC, HP * hf + HP)
                            if a < e:
                                last = nc.tensor.matmul(slot[64 * hf:64 * hf + 64, 0, a - t0:e - t0],
                                                        wo[:], yn[x][:, a - t0:e - t0], start=True, stop=True)
                        last.then_inc(o_ready, 1)

                    pe.wait_ge(stacks_in[g], S_IN * third + S_IN)
                    pe.wait_ge(rest_in[b], R_IN * half + R_IN)
                    n = 0
                    for kind, what in order:
                        if first and kind in "wdro" and what < 0:
                            n += kind == "o"
                            continue
                        if kind in "sto":
                            slot_free(n)
                            slot = ps[n % 2]
                            n += 1
                        if kind == "s":
                            score(slot, what)
                        elif kind == "m":
                            if what == 0:
                                pe.wait_ge(stacks_in[(g + 1) % 3], S_IN * (third + (g == 2)) + S_IN)
                            top_unit(what, i + 1, (g + 1) % 3, True)
                        elif kind == "t":
                            turn(slot, i + 1)
                        elif kind == "w":
                            weigh(what)
                        elif kind == "d":
                            denominators(what)
                        elif kind == "o":
                            project(slot, what)

                image.eng = pe
                every_image(image, before)

            @block.scalar
            def _(act):
                act.preload_act_table_set("natural_log_exp_and_others")

                def image(i, b, half, g, third, order, first):
                    n = 0
                    for kind, u in order:
                        if kind == "d" and not (first and u < 0):
                            x = (NTC * b + u) % 2
                            act.wait_ge(den_ready, NTC * i + u + 1)
                            nc.scalar.activation(lden[x], av[x][:, 0:TC], ACT.Ln).then_inc(ln_done, 1)
                            act.wait_ge(ln_done, NTC * i + u + 1)
                            act.wait_ge(y_normed, NTC * i + u + 1)
                            nc.scalar.activation(rec[x], lden[x], ACT.Exp, scale=-1.0).then_inc(rec_ready, 1)
                        if kind == "s":
                            q, s, t0 = pieces[u // 2]
                            kv, w, m = u % 2, TC * (q + 1) - t0, keys(s)
                            act.wait_ge(scored, NEX * i + u + 1)
                            if kv == 0:
                                act.wait_ge(summed, NPC * i + u // 2 + 1)
                            nc.scalar.activation(prob[(u // 2) % 3][0:m, 2 * kv:2 * kv + 2, 0:w],
                                                 ps[n % 2][0:m, :, 0:w], ACT.Exp, scale=0.25).then_inc(expd, 1)
                        n += kind in "sto"

                image.eng = act
                every_image(image, lambda: act.sem_inc(expd, NEX))

            @block.vector
            def _(dve):
                def reduce(n, x):
                    t, h, z, s, w = units[n]
                    dve.wait_ge(mscored, NU * x + n + 1)
                    if t < 4:
                        out = mx[:, t, h:h + 1]
                    elif t < 8:
                        out = m2[:, t - 4, h, z:z + 1]
                    else:
                        out = m3[:, 3 * h + z:3 * h + z + 1]
                    nc.vector.tensor_reduce(out, mp[n % 2][0:TB, 0:w], axis=AX.X, op=ALU.max).then_inc(reduced, 1)

                def join(x):
                    dve.wait_ge(reduced, NU * x + NU)
                    nc.vector.tensor_reduce(mx[:, 4:8, :], m2[:], axis=AX.X, op=ALU.max).then_inc(joined, 1)
                    nc.vector.tensor_reduce(mx[:, 8, :], m3[:].rearrange("p (h c) -> p h c", c=3),
                                            axis=AX.X, op=ALU.max).then_inc(joined, 1)
                    dve.wait_ge(joined, 2 * x + 2)
                    mT = mx[:].rearrange("p t h -> p h t")
                    nc.vector.tensor_scalar(nmh[:], mT, -1.0, None, ALU.mult).then_inc(hi, 1)
                    dve.wait_ge(hi, 2 * x + 1)
                    nc.vector.tensor_copy(nm[:, 0, :, :], nmh[:]).then_inc(hi, 1)
                    nc.vector.scalar_tensor_tensor(nm[:, 1, :, :], mT, -1.0, nmh[:], ALU.mult, ALU.subtract)\
                        .then_inc(lo, 1)

                def copy_turned(slot, x, b):
                    dve.wait_ge(turned, x + 1)
                    nc.vector.tensor_copy(nmT[b][:], slot[0:NMX, 0, 0:TB]).then_inc(nm_copied, 1)

                def before():
                    dve.sem_inc(summed, 3)
                    dve.sem_inc(rec_done, 2)
                    dve.sem_inc(o_added, NTC)
                    for n in range(NU):
                        reduce(n, 0)
                    join(0)
                    copy_turned(ps[1], 0, 0)

                def image(i, b, half, g, third, order, first):
                    n = 0
                    for kind, what in order:
                        slot = ps[n % 2]
                        n += kind in "sto"
                        if first and kind in "wdro" and what < 0:
                            continue
                        if kind == "m":
                            reduce(what, i + 1)
                        elif kind == "j":
                            join(i + 1)
                        elif kind == "t":
                            copy_turned(slot, i + 1, 1 - b)
                        elif kind == "w" and what % NPC in ends:
                            q = pieces[what][0] if what >= 0 else -1
                            x = (NTC * b + q) % 2
                            dve.wait_ge(summed, NPC * i + what + 1 + 3)
                            dve.wait_ge(y_normed, NTC * i + q + 1)
                            nc.vector.tensor_copy(yv[x], av[x][:, 0:TC]).then_inc(y_copied, 1)
                        elif kind == "r":
                            x = (NTC * b + what) % 2
                            dve.wait_ge(rec_ready, NTC * i + what + 1)
                            nc.vector.tensor_tensor(lden[x], rec[x], av[x][:, 0:TC], ALU.mult).then_inc(rec_done, 1)
                        elif kind == "o":
                            dve.wait_ge(o_ready, NTC * i + what + 1)
                            img, t0 = (i if what >= 0 else i - 1), TC * (what % NTC)
                            flatx = XN[:, img, :, :].rearrange("p c n -> p (c n)")
                            for hf in range(2):
                                a, e = max(t0, HP * hf), min(t0 + TC, HP * hf + HP)
                                if a < e:
                                    r, cs = slice(64 * hf, 64 * hf + 64), slice(a - HP * hf, e - HP * hf)
                                    last = nc.vector.tensor_tensor(flatx[r, cs], flatx[r, cs],
                                                                   slot[r, 0, a - t0:e - t0], ALU.add)
                            last.then_inc(o_added, 1)

                image.eng = dve
                every_image(image, before)
                dve.wait_ge(o_added, NTC * B + NTC)

            @block.gpsimd
            def _(pool):
                def image(i, b, half, g, third, order, first):
                    for kind, q in order:
                        if kind == "r" and not (first and q < 0):
                            x = (NTC * b + q) % 2
                            pool.wait_ge(rec_done, NTC * i + q + 3)
                            nc.gpsimd.tensor_tensor(lden[x], two[:], lden[x], op=ALU.subtract).then_inc(newton, 1)
                            nc.gpsimd.tensor_tensor(rec[x], rec[x], yv[x], op=ALU.mult).then_inc(newton, 1)
                            pool.wait_ge(newton, 2 * (NTC * i + q) + 2)
                            nc.gpsimd.tensor_tensor(yn[x], rec[x], lden[x], op=ALU.mult).then_inc(y_normed, 1)

                image.eng = pool
                every_image(image, lambda: pool.sem_inc(y_normed, 2))


def router_phase(nc, P, A, FL, cst, we_d):
    E2 = 2 * NE
    NB_ = 5
    with ExitStack() as c:
        rw, ln2 = P.sb(c, "rw", [128, E2]), P.sb(c, "ln2r", [128, 1])
        lg = [P.sb(c, f"lg{k}", [E2, NB_ * RB]) for k in range(2)]
        LT = P.sb(c, "LT", [RB, B, NB_ * E2])
        load_phase(nc, P, [(rw[:], A["rw"]), (ln2[:], A["ln2"])], "router")
        w_scaled, lg_ready, lg_copied, turned, lt_copied = (P.sem(f"rt_{x}") for x in
                                                            ("w_scaled", "lg_ready", "lg_copied", "turned", "lt_copied"))
        passed = P.sem("rt_passed")
        with ExitStack() as cc:
            lp = [P.ps(cc, f"rt_lp{k}", [E2, 2, 512]) for k in range(2)]
            tp = [P.ps(cc, f"rt_tp{k}", [RB, 512]) for k in range(2)]
            with nc.Block() as block:
                @block.vector
                def _(dve):
                    nc.vector.tensor_scalar(rw[:], rw[:], ln2[:, 0:1], None, ALU.mult).then_inc(w_scaled, 1)
                    for k in range(2):
                        nc.vector.memset(lg[k][:, HP:NB_ * RB], 0.0).then_inc(lg_copied, 1)
                    dve.sem_inc(lt_copied, 2)
                    with dve.Fori(0, B // 2) as j:
                        for k in range(2):
                            i = 2 * j + k
                            dve.wait_ge(lg_ready, i + 1)
                            dve.wait_ge(lt_copied, i + 1)
                            nc.vector.tensor_copy(lg[k][:, 0:HP].rearrange("p (c n) -> p c n", c=2),
                                                  lp[k][:, :, 0:CH]).then_inc(lg_copied, 1)

                @block.tensor
                def _(pe):
                    pe.wait_ge(w_scaled, 1)
                    with pe.Fori(0, B // 2) as j:
                        for k in range(2):
                            i = 2 * j + k
                            pe.wait_ge(lg_copied, i + 1)
                            mm2(nc, lp[k], rw[:], FL[:, i, :, :]).then_inc(lg_ready, 1)
                        for k in range(2):
                            i = 2 * j + k
                            pe.wait_ge(lg_copied, i + 3)
                            wait_alone(pe, lt_copied, i + 1, passed)
                            for b in range(NB_):
                                last = nc.tensor.transpose(tp[k][:, E2 * b:E2 * b + E2], lg[k][:, RB * b:RB * b + RB],
                                                           cst["ident"][0:E2, 0:E2])
                            last.then_inc(turned, 1)

                @block.scalar
                def _(act):
                    with act.Fori(0, B // 2) as j:
                        for k in range(2):
                            i = 2 * j + k
                            act.wait_ge(turned, i + 1)
                            nc.scalar.activation(LT[:, i, :], tp[k][:, 0:NB_ * E2], ACT.Copy).then_inc(lt_copied, 1)
        NG = B * NB_ * 2
        with ExitStack() as cc:
            m = P.sb(cc, "rt_m", [RB, NG, 1])
            den = P.sb(cc, "rt_den", [RB, NG, 1])
            top = [P.sb(cc, f"rt_top{n}", [RB, NG, 1]) for n in range(2)]
            hot = [P.sb(cc, f"rt_hot{n}", [RB, NG, NE]) for n in range(2)]
            rank = P.sb(cc, "rt_rank", [RB, NE])
            work = P.sb(cc, "rt_work", [RB, NG, NE])
            step, e_ready, e_done = (P.sem(f"rt_{x}") for x in ("step", "e_ready", "e_done"))
            pr = LT[:].rearrange("p b (g e) -> p (b g) e", e=NE)

            def wide(x):
                return x[:].broadcast_to([RB, NG, NE])

            load_phase(nc, P, [(rank[:], A["rank"])], "rank")
            with nc.Block() as block:
                @block.scalar
                def _(act):
                    act.preload_act_table_set("exp_and_others")
                    act.wait_ge(e_ready, 1)
                    nc.scalar.activation(pr, pr, ACT.Exp).then_inc(e_done, 1)

                @block.vector
                def _(dve):
                    n = [0]

                    def then(ins):
                        n[0] += 1
                        ins.then_inc(step, 1)
                        dve.wait_ge(step, n[0])

                    v = nc.vector
                    rk = rank[:].rearrange("p (z e) -> p z e", z=1).broadcast_to([RB, NG, NE])
                    then(v.tensor_reduce(m[:], pr, axis=AX.X, op=ALU.max))
                    v.tensor_tensor(pr, pr, wide(m), ALU.subtract).then_inc(e_ready, 1)
                    dve.wait_ge(e_done, 1)
                    then(v.tensor_reduce(den[:], pr, axis=AX.X, op=ALU.add))
                    then(v.reciprocal(den[:], den[:]))
                    then(v.tensor_tensor(pr, pr, wide(den), ALU.mult))
                    for r in range(2):
                        then(v.tensor_reduce(top[r][:], pr, axis=AX.X, op=ALU.max))
                        then(v.tensor_tensor(work[:], pr, wide(top[r]), ALU.is_equal))
                        then(v.tensor_tensor(work[:], work[:], rk, ALU.mult))
                        then(v.tensor_reduce(m[:], work[:], axis=AX.X, op=ALU.max))
                        then(v.tensor_tensor(hot[r][:], work[:], wide(m), ALU.is_equal))
                        if r == 0:
                            then(v.scalar_tensor_tensor(pr, hot[0][:], -2.0, pr, ALU.mult, ALU.add))
                    then(v.tensor_tensor(den[:], top[0][:], top[1][:], ALU.add))
                    then(v.tensor_scalar(den[:], den[:], 1e-9, None, ALU.add))
                    then(v.reciprocal(den[:], den[:]))
                    for r in range(2):
                        then(v.tensor_tensor(top[r][:], top[r][:], den[:], ALU.mult))
                        then(v.tensor_tensor(hot[r][:], hot[r][:], wide(top[r]), ALU.mult))
                    then(v.tensor_tensor(pr, hot[0][:], hot[1][:], ALU.add))
        with ExitStack() as cc:
            NRW = NB_ * E2
            WT = P.sb(cc, "WT", [NRW, B, RB])
            rest = P.sb(cc, "WT_rest", [NRW, B, RB])
            parts = P.sb(cc, "WT_parts", [NRW, 3, B, RB], BF16)
            st = P.sb(cc, "rt_static", [RB, 2, NRW])
            wp = [P.ps(cc, f"rt_wp{k}", [NRW, RB]) for k in range(2)]
            staged, turned2, copied, stored = (P.sem(f"we_{x}") for x in ("staged", "turned", "copied", "stored"))
            cut_done = P.sem("we_cut")
            with nc.Block() as block:
                @block.scalar
                def _(act):
                    with act.Fori(0, B // 2) as j:
                        for k in range(2):
                            i = 2 * j + k
                            act.wait_ge(copied, i + 1)
                            nc.scalar.activation(st[:, k, :], LT[:, i, :], ACT.Copy).then_inc(staged, 1)

                @block.tensor
                def _(pe):
                    with pe.Fori(0, B // 2) as j:
                        for k in range(2):
                            i = 2 * j + k
                            pe.wait_ge(staged, i + 1)
                            nc.tensor.transpose(wp[k][:], st[:, k, :], cst["ident"][0:RB, 0:RB]).then_inc(turned2, 1)

                @block.vector
                def _(dve):
                    dve.sem_inc(copied, 2)
                    with dve.Fori(0, B // 2) as j:
                        for k in range(2):
                            i = 2 * j + k
                            dve.wait_ge(turned2, i + 1)
                            nc.vector.tensor_copy(WT[:, i, :], wp[k][:]).then_inc(copied, 1)
                    dve.wait_ge(copied, B + 2)
                    cut(nc, cut_done, dve, WT[:], parts[:, 0], rest[:], parts[:, 1], parts[:, 2], 0)

                @block.sync
                def _(sp):
                    for a, n in ((0, 1), (1, 3), (2, 4)):
                        sp.wait_ge(cut_done, n)
                        for b in range(NB_):
                            sp.dma_start(we_d[a, :, :, RB * b:RB * b + RB], parts[E2 * b:E2 * b + E2, a, :, :])\
                                .then_inc(stored, 16)
                    sp.wait_ge(stored, 16 * 3 * NB_)


def expert_phase(nc, P, A, XN, FL, h4_d, we_d, out_d):
    with ExitStack() as c:
        ws = [P.sb(c, f"ex_w{n}", [128, 3, NTL * 128], BF16) for n in range(2)]
        w2 = P.sb(c, "ex_w2", [128, NTL, D])
        spread = P.sb(c, "ex_spread", [3 * NE, NTL * 128], BF16)
        w_scaled, w_cut, spread_cast = (P.sem(f"ex_{x}") for x in ("w_scaled", "w_cut", "spread_cast"))
        with ExitStack() as cc:
            raw = [P.sb(cc, f"ex_raw{n}", [128, NTL * 128]) for n in range(2)]
            rest = P.sb(cc, "ex_rest", [128, NTL * 128])
            third = P.sb(cc, "ex_third", [128, NTL * 128], BF16)
            spread32 = P.sb(cc, "ex_spread32", [3 * NE, NTL * 128])
            ln2 = P.sb(cc, "ln2e", [128, 1])
            load_phase(nc, P, [(raw[0][:], A["ex_w1"]), (raw[1][:], A["ex_w3"]), (ln2[:], A["ln2"]),
                               (w2[:].rearrange("p t m -> p (t m)"), A["ex_w2"]), (spread32[:], A["spread"])], "ex")
            with nc.Block() as block:
                @block.vector
                def _(dve):
                    nc.vector.tensor_copy(spread[:], spread32[:]).then_inc(spread_cast, 1)
                    for n in range(2):
                        nc.vector.tensor_scalar(raw[n][:], raw[n][:], ln2[:, 0:1], None, ALU.mult).then_inc(w_scaled, 1)
                    dve.wait_ge(w_scaled, 2)
                    n = 0
                    for w, r in zip(ws, raw):
                        n = cut(nc, w_cut, dve, r[:], w[:, 0, :], rest[:], w[:, 1, :], third[:], n)
                        nc.vector.tensor_copy(w[0:64, 2, :], third[0:64, :])
                        nc.vector.tensor_copy(w[64:128, 2, :], w[64:128, 0, :]).then_inc(w_cut, 1)
                        n += 1
                        dve.wait_ge(w_cut, n)
        fl = [P.sb(c, f"ex_fl{n}", [128, 3, HP], BF16) for n in range(2)]
        fr = P.sb(c, "ex_fr", [128, 2, CH])
        xs = [P.sb(c, f"ex_xs{n}", [128, 2, TP], BF16) for n in range(2)]
        we = [P.sb(c, f"ex_we{n}", [3 * NE, TP], BF16) for n in range(2)]
        sl = [P.sb(c, f"ex_sl{n}", [128, 2, CH]) for n in range(2)]
        hu = [P.sb(c, f"ex_hu{n}", [128, 2, CH]) for n in range(4)]
        h4 = [P.sb(c, f"ex_h4{n}", [128, HP]) for n in range(2)]
        gp, up, wp, y = (P.ps(c, f"ex_{x}p", [128, 2, 512]) for x in ("g", "u", "w", "y"))
        part_done, xs_ready = P.sem("ex_part_done"), [P.sem(f"ex_xs_ready{n}") for n in range(2)]
        h4_ready = [P.sem(f"ex_h4_ready{n}") for n in range(2)]
        g_ready, u_ready, w_ready = (P.sem(f"ex_{x}_ready") for x in ("g", "u", "w"))
        silu_done, gated, weighted = (P.sem(f"ex_{x}") for x in ("silu_done", "gated", "weighted"))
        down, y_read, r_ready, image_read = (P.sem(f"ex_{x}") for x in ("down", "y_read", "r_ready", "image_read"))
        stored = [P.sem(f"ex_stored{n}") for n in range(2)]
        passed = P.sem("ex_passed")
        outv = out_d.rearrange("p (b n) -> p b n", b=B)
        h4v = h4_d.rearrange("p (b n) -> p b n", b=B)
        NLD = 16 * (8 + 6)
        NU = 2 * NTL
        with nc.Block() as block:
            @block.gpsimd
            def _(pool):
                for k in range(2):
                    pool.sem_inc(xs_ready[k], NLD)
                with pool.Fori(0, B // 2) as j:
                    for k in range(2):
                        i = 2 * j + k
                        f = [fl[k][:, m, :].rearrange("p (c n) -> p c n", c=2) for m in range(3)]
                        wait_alone(pool, xs_ready[k], NLD * j + NLD, passed)
                        nc.gpsimd.tensor_copy(f[0], FL[:, i, :, :]).then_inc(part_done, 1)
                        wait_alone(pool, part_done, 4 * i + 1, passed)
                        nc.gpsimd.tensor_tensor(fr[:], FL[:, i, :, :], f[0], op=ALU.subtract).then_inc(part_done, 1)
                        wait_alone(pool, part_done, 4 * i + 2, passed)
                        nc.gpsimd.tensor_copy(f[1], fr[:]).then_inc(part_done, 1)
                        wait_alone(pool, part_done, 4 * i + 3, passed)
                        nc.gpsimd.tensor_tensor(f[2], fr[:], f[1], op=ALU.subtract).then_inc(part_done, 1)
                        wait_alone(pool, part_done, 4 * i + 4, passed)
                        wait_alone(pool, h4_ready[k], 16 * j + 16, passed)
                        h4c = h4[k][:].rearrange("p (c n) -> p c n", c=2)
                        nc.gpsimd.tensor_tensor(h4c, XN[:, i, :, :], h4c, op=ALU.add).then_inc(r_ready, 1)

            @block.sync
            def _(sp):
                with sp.Fori(0, B // 2) as j:
                    for k in range(2):
                        i = 2 * j + k
                        sp.wait_ge(image_read, i + 1)
                        for a in range(3):
                            for h in range(2):
                                sp.dma_start(we[k][NE * a:NE * a + NE, HP * h:HP * h + HP],
                                             we_d[a, NE * h:NE * h + NE, i, 0:HP]).then_inc(xs_ready[k], 16)
                        sp.wait_ge(stored[k], 16 * j + 16)
                        sp.dma_start(h4[k][:], h4v[:, i, :]).then_inc(h4_ready[k], 16)
                        sp.wait_ge(part_done, 4 * i + 4)
                        for s, r, a in ((0, 0, 0), (0, 64, 1), (1, 0, 0), (1, 64, 2)):
                            for h in range(2):
                                sp.dma_start(xs[k][r:r + 64, s, HP * h:HP * h + HP],
                                             fl[k][64 * h:64 * h + 64, a, :]).then_inc(xs_ready[k], 16)

            @block.tensor
            def _(pe):
                pe.sem_inc(image_read, 2)
                with pe.Fori(0, B // 2) as j:
                    for k in range(2):
                        i = 2 * j + k
                        pe.wait_ge(xs_ready[k], NLD * j + 2 * NLD)

                        def three(out, w, t, h):
                            for q in range(2):
                                s = HP * h + CH * q
                                for m in range(3):
                                    last = nc.tensor.matmul(out[:, q, 0:CH], w[:, m, 128 * t:128 * t + 128],
                                                            xs[k][:, m // 2, s:s + CH], start=m == 0, stop=m == 2)
                            return last

                        def second(t, q):
                            if q == 0:
                                pe.wait_ge(weighted, NU * i + 2 * t + 2 + 4)
                                if t == 0:
                                    pe.wait_ge(y_read, i + 1)
                            for h in range(2):
                                last = nc.tensor.matmul(y[64 * h:64 * h + 64, q, 0:CH], w2[:, t, :],
                                                        hu[2 * (t % 2) + h][:, q, :], start=t == 0, stop=t == NTL - 1)
                            if q == 1:
                                last.then_inc(down, 1)

                        for t in range(NTL):
                            for h in range(2):
                                n = NU * i + 2 * t + h
                                pe.wait_ge(silu_done, n + 1)
                                three(gp, ws[0], t, h).then_inc(g_ready, 1)
                                pe.wait_ge(gated, n + 2)
                                three(up, ws[1], t, h).then_inc(u_ready, 1)
                                pe.wait_ge(weighted, n + 4)
                                for q in range(2):
                                    last = nc.tensor.matmul(wp[:, q, 0:CH], spread[:, 128 * t:128 * t + 128],
                                                            we[k][:, HP * h + CH * q:HP * h + CH * q + CH],
                                                            start=True, stop=True)
                                last.then_inc(w_ready, 1)
                                if t >= 1:
                                    second(t - 1, h)
                        pe.wait_ge(w_ready, NU * i + NU)
                        pe.sem_inc(image_read, 1)
                        for q in range(2):
                            second(NTL - 1, q)

            @block.scalar
            def _(act):
                act.preload_act_table_set("silu_and_others")
                act.sem_inc(silu_done, 1)
                for k in range(2):
                    act.sem_inc(stored[k], 16)
                with act.Fori(0, B // 2) as j:
                    for k in range(2):
                        i = 2 * j + k
                        for u in range(NU):
                            act.wait_ge(g_ready, NU * i + u + 1)
                            act.wait_ge(gated, NU * i + u + 1)
                            nc.scalar.activation(sl[u % 2][:], gp[:, :, 0:CH], ACT.Silu).then_inc(silu_done, 1)
                        act.wait_ge(y_read, i + 2)
                        act.dma_start(outv[:, i, :], h4[k][:]).then_inc(stored[k], 16)
                for k in range(2):
                    act.wait_ge(stored[k], 16 * (B // 2) + 16)

            @block.vector
            def _(dve):
                dve.sem_inc(gated, 2)
                dve.sem_inc(weighted, 4)
                dve.sem_inc(y_read, 1)
                dve.sem_inc(down, 2)
                with dve.Fori(0, B // 2) as j:
                    for k in range(2):
                        i = 2 * j + k
                        for u in range(NU):
                            n = NU * i + u
                            t, h = u // 2, u % 2
                            buf = hu[2 * (t % 2) + h]
                            dve.wait_ge(silu_done, n + 2)
                            dve.wait_ge(u_ready, n + 1)
                            if h == 0:
                                dve.wait_ge(down, NTL * i + t + 1)
                            nc.vector.tensor_tensor(buf[:], sl[u % 2][:], up[:, :, 0:CH], ALU.mult).then_inc(gated, 1)
                            dve.wait_ge(gated, n + 3)
                            dve.wait_ge(w_ready, n + 1)
                            nc.vector.tensor_tensor(buf[:], buf[:], wp[:, :, 0:CH], ALU.mult).then_inc(weighted, 1)
                        dve.wait_ge(down, NTL * i + NTL + 2)
                        dve.wait_ge(r_ready, i + 1)
                        h4c = h4[k][:].rearrange("p (c n) -> p c n", c=2)
                        nc.vector.tensor_tensor(h4c, h4c, y[:, :, 0:CH], ALU.add).then_inc(y_read, 1)


def build(nc, A, out_d):
    with ExitStack() as ctx:
        P = Place(nc)
        H = P.sb(ctx, "H", [128, B, 2, CH])
        XN = P.sb(ctx, "XN", [128, B, 2, CH])
        ident, centre, average = (P.sb(ctx, n, [128, 128]) for n in ("ident", "centre", "average"))
        ident16 = P.sb(ctx, "ident16", [128, 128], BF16)
        cst = {"ident": ident, "centre": centre[:], "average": average[:], "ident16": ident16[:]}

        def dram(name, shape, dt=F32):
            return nc.dram_tensor(name, shape, dt, kind="Internal").ap()

        wr_rows, sel_rows = dram("wr_rows", [B, 2, HP]), dram("sel_rows", [B, 2, HP])
        h4_d = dram("h4_d", [128, B * HP])
        parts_d = dram("parts_d", [B, 3, (NH + NKV) * HD, TP], BF16)
        va_d = dram("va_d", [B, 128, NTB * NH * 32])
        we_d = dram("we_d", [3, 2 * NE, B, 5 * RB], BF16)

        load_phase(nc, P, [(ident[:], A["ident"]), (centre[:], A["centre"]), (average[:], A["average"])], "common")
        ident_cast = P.sem("ident_cast")
        with nc.Block() as block:
            @block.vector
            def _(dve):
                nc.vector.tensor_copy(ident16[:], ident[:]).then_inc(ident_cast, 1)
        embed_phase(nc, P, A, H)
        P.clear()
        norm_phase(nc, P, "n1", cst, H, XN, 1e-5, True)
        P.clear()
        gate_phase(nc, P, A, H, XN)
        P.clear()
        norm_phase(nc, P, "n2", cst, H, XN, 1e-5, True)
        P.clear()
        token_weight_phase(nc, P, A, XN, wr_rows)
        P.clear()
        mlp_phase(nc, P, A, H, XN, wr_rows, sel_rows)
        P.clear()
        norm_phase(nc, P, "n3", cst, H, XN, 1e-5, True)
        P.clear()
        rnn_phase(nc, P, A, H, XN)
        P.clear()
        norm_phase(nc, P, "n4", cst, H, XN, 1e-5, True, spill=h4_d)
        P.clear()
        norm_phase(nc, P, "n5", cst, XN, H, 1e-6, False)
        P.clear()
        qkv_phase(nc, P, A, H, cst, parts_d, va_d)
        P.clear()
        attention_phase(nc, P, A, XN, H, parts_d, va_d, cst)
        P.clear()
        norm_phase(nc, P, "n6", cst, XN, H, 1e-6, False)
        P.clear()
        router_phase(nc, P, A, H, cst, we_d)
        P.clear()
        expert_phase(nc, P, A, XN, H, h4_d, we_d, out_d)
        P.clear()


def diag2(w):
    n, m = w.shape
    z = np.zeros((2 * n, 2 * m), w.dtype)
    z[:n, :m], z[n:, m:] = w, w
    return z


def layouts(x):
    f = {k: np.asarray(v) for k, v in x.items()}
    r = {}

    def col(v):
        return np.ascontiguousarray(np.tile(v.reshape(-1), 2)[:, None])

    n = 224 // 7
    p = f["x"].reshape(B, n, 7, n, 7).transpose(2, 4, 0, 1, 3).reshape(PD, B, n * n)
    z = np.zeros((PD, B, TP), np.float32)
    z[:, :, 1:T] = p
    r["patches"] = z.reshape(PD, B, 2, HP).transpose(2, 0, 1, 3).reshape(2 * PD, B * HP)
    r["wtok"] = diag2(f["L0_tok_W"].T)
    z = np.zeros((D, TP), np.float32)
    z[:, 0] = f["cls_tok"].reshape(-1)
    z[:, 1:T] = f["L0_tok_pos"][0].T
    r["pos"] = z.reshape(D, 2, HP).transpose(1, 0, 2).reshape(128, HP)
    r["tokb"] = col(f["L0_tok_b"])
    r["wg"], r["wo"] = diag2(f["L0_attn_wg"]), diag2(f["L0_attn_wo"])
    r["gnb"], r["attn_b"] = col(f["L0_attn_gn_bias"]), col(f["L0_attn_bias"])
    r["wr"] = diag2(np.repeat(f["L0_ffn_wr"], D, axis=1))
    r["br"] = np.repeat(f["L0_ffn_br"], 128)[:, None]
    w1, w2 = f["L0_ffn_w1"], f["L0_ffn_w2"]
    r["w1"] = np.stack([diag2(w1[:, D * m:D * m + D]) for m in range(4)], 1)
    r["w2"] = np.stack([diag2(w2[D * m:D * m + D]) for m in range(4)], 1)
    r["b1"] = np.tile(f["L0_ffn_b1"].reshape(4, D).T, (2, 1))
    r["b2"] = col(f["L0_ffn_b2"])
    r["wih"], r["whh"] = diag2(f["L1_attn_W_ih"].T), diag2(f["L1_attn_W_hh"].T)
    r["bih"], r["bhh"] = col(f["L1_attn_b_ih"]), col(f["L1_attn_b_hh"])
    wqkv = np.concatenate([f["L1_ffn_wq"].T, f["L1_ffn_wk"].T, f["L1_ffn_wv"].T], 1)
    turn = np.concatenate([np.roll(np.arange(HD), -HD // 2) + HD * h for h in range(8)])
    both = np.stack([wqkv, wqkv[:, turn]], 1)
    z = np.zeros((2, D, 2, 2, 128), np.float32)
    z[0, :, 0], z[1, :, 1] = both, both
    r["wqkv"] = z.reshape(128, 512)
    r["ln1"], r["ln2"] = col(f["L1_ffn_ln1_w"]), col(f["L1_ffn_ln2_w"])
    wo = f["L1_ffn_wo"].T
    z = np.zeros((NH, 32, D), np.float32)
    z[:, 0:HD] = wo.reshape(NH, HD, D)
    r["attn_wo"] = z.reshape(128, D)
    r["rw"] = diag2(f["L1_ffn_router_w"].T)
    for name in ("w1", "w3"):
        w = np.zeros((NTL * 128, D), np.float32)
        w[0:NE * HID] = f[f"L1_ffn_{name}"].reshape(NE * HID, D)
        r[f"ex_{name}"] = np.tile(w.T, (2, 1))
    w = np.zeros((NTL * 128, D), np.float32)
    w[0:NE * HID] = f["L1_ffn_w2"].transpose(0, 2, 1).reshape(NE * HID, D)
    r["ex_w2"] = w.reshape(NTL, 128, D).transpose(1, 0, 2).reshape(128, NTL * D)
    return {k: np.ascontiguousarray(v) for k, v in r.items()}


def tables():
    r = {"ident": np.eye(128, dtype=np.float32)}
    one = np.zeros((128, 128), np.float32)
    one[:D, :D] = one[D:, D:] = 1.0 / D
    r["average"], r["centre"] = one, np.eye(128, dtype=np.float32) - one
    inv = 1.0 / 10000.0 ** (np.arange(0, HD, 2, dtype=np.float32) / HD)
    ang = np.outer(np.arange(TP, dtype=np.float32), inv)
    ang = np.concatenate([ang, ang], -1).T
    sign = np.where(np.arange(HD) < HD // 2, -1.0, 1.0).astype(np.float32)[:, None]
    r["cos"] = np.tile(np.cos(ang), (NH + NKV, 1)).astype(np.float32)
    r["sin"] = np.tile(np.sin(ang) * sign, (NH + NKV, 1)).astype(np.float32)
    a = np.arange(128)
    r["mask1"] = np.where(a[None, :TB] > a[:TB, None], NEG, 0.0).astype(np.float32)
    r["mask2"] = np.where(a[:, None] > a[None, :], NEG, 0.0).astype(np.float32)
    z = np.zeros((128, 128), np.float32)
    for h in range(NH):
        z[32 * h + HD, 32 * h:32 * h + 32] = 1.0
    r["attn_sel"] = z
    z = np.zeros((NE, NTL * 128), np.float32)
    for e in range(NE):
        z[e, HID * e:HID * e + HID] = 1.0
    r["spread"] = np.tile(z, (3, 1))
    r["rank"] = np.tile(np.arange(NE, 0, -1, dtype=np.float32), (RB, 1))
    return r


def kernel(**inputs):
    import concourse.bacc as _bacc
    from concourse.bass_utils import run_bass_kernel_spmd as _run

    nc = _bacc.Bacc("TRN2", target_bir_lowering=False, num_devices=1)
    arrays = {**layouts(inputs), **tables()}
    A = {n: nc.dram_tensor(f"in_{n}", a.shape, mybir.dt.from_np(a.dtype), kind="ExternalInput").ap()
         for n, a in arrays.items()}
    out_d = nc.dram_tensor("out_0", (128, B * HP), F32, kind="ExternalOutput").ap()
    build(nc, A, out_d)
    r = _run(nc, [{f"in_{n}": a for n, a in arrays.items()}], core_ids=[0])
    o = r.results[0]["out_0"].reshape(2, D, B, HP).transpose(2, 0, 3, 1).reshape(B, TP, D)
    return np.ascontiguousarray(o[:, :T])
```
